# Optimizing a Trainium2 kernel written in Bass

```python
import numpy as np
import jax
import jax.numpy as jnp

def _softmax(x, axis=-1):
    return jax.nn.softmax(x, axis=axis)

def _gelu(x):
    return jax.nn.gelu(x, approximate=True)

def _silu(x):
    return jax.nn.silu(x)

def _sigmoid(x):
    return jax.nn.sigmoid(x)

def _layernorm(x, axis=-1, eps=1e-05):
    m = jnp.mean(x, axis=axis, keepdims=True)
    v = jnp.var(x, axis=axis, keepdims=True)
    return (x - m) / jnp.sqrt(v + eps)

def _scatter_add(tgt, idx, src, axis=0):
    return tgt.at[idx].add(src)

def _segment_sum(src, seg, n):
    return jax.ops.segment_sum(src, seg, n)
kernel_name = 'mk_cond_seq_d2_seqx_r8_4e9589'

def setup_inputs(seed: int=0):
    np.random.seed(seed)
    _w = jnp.asarray

    def _rec_inputs():
        import jax
        import jax.numpy as jnp
        _rk = jax.random.key(seed)
        x = 1.648e-05 + 1 * jax.random.normal(jax.random.fold_in(_rk, 1), (16, 128, 144), jnp.float32)
        _lenS = 128 - jax.random.randint(jax.random.fold_in(_rk, 7), (16,), 0, max(1, 128 // 4) + 1, jnp.int32)
        _lenS2 = 128 - jax.random.randint(jax.random.fold_in(_rk, 8), (16,), 0, max(1, 128 // 4) + 1, jnp.int32)
        cond_1152 = 0.00914911 + 1.00357 * jax.random.normal(jax.random.fold_in(_rk, 11), (16, 144), jnp.float32)
        return (x, cond_1152)
    x, cond_1152 = _rec_inputs()

    def _L0_cond_setup():
        import jax, jax.numpy as jnp
        import numpy as np
        NUM_HEADS = 16
        NUM_EXPERTS = 4
        TOP_K = 2
        LN_EPS = 1e-06

        def _ln(h):
            mu = jnp.mean(h, axis=-1, keepdims=True)
            var = jnp.var(h, axis=-1, keepdims=True)
            return (h - mu) * jax.lax.rsqrt(var + LN_EPS)

        def _modulate(h, shift, scale):
            return h * (1.0 + scale[:, None, :]) + shift[:, None, :]
        key = jax.random.key(seed)
        ks = jax.random.split(key, 12)
        B, N, C = (8, 128, 144)
        H = 4 * C
        E = NUM_EXPERTS
        s = 0.02
        return {'x': jax.random.normal(ks[0], (B, N, C), jnp.float32), 'c': jax.random.normal(ks[1], (B, C), jnp.float32), 'w_adaln': jax.random.normal(ks[2], (C, 6 * C), jnp.float32) * s, 'b_adaln': jnp.zeros((6 * C,), jnp.float32), 'w_qkv': jax.random.normal(ks[3], (C, 3 * C), jnp.float32) * s, 'b_qkv': jnp.zeros((3 * C,), jnp.float32), 'w_proj': jax.random.normal(ks[4], (C, C), jnp.float32) * s, 'b_proj': jnp.zeros((C,), jnp.float32), 'w_gate': jax.random.normal(ks[5], (C, E), jnp.float32) * s, 'w1': jax.random.normal(ks[6], (E, C, H), jnp.float32) * s, 'b1': jnp.zeros((E, H), jnp.float32), 'w2': jax.random.normal(ks[7], (E, H, C), jnp.float32) * s, 'b2': jnp.zeros((E, C), jnp.float32)}
    _L0_cond_all = _L0_cond_setup()
    _L0_cond_in = {k: v for k, v in _L0_cond_all.items() if k in ('w_adaln', 'b_adaln', 'w_qkv', 'b_qkv', 'w_proj', 'b_proj', 'w_gate', 'w1', 'b1', 'w2', 'b2')}
    del _L0_cond_all

    def _L1_cond_setup():
        import jax, jax.numpy as jnp
        import numpy as np
        B, S, D = (8, 128, 144)
        H = 16
        HD = D // H
        HID = int(D * 4.0)
        LN_EPS = 1e-05

        def layer_norm(x, w, b):
            m = jnp.mean(x, axis=-1, keepdims=True)
            v = jnp.mean(jnp.square(x - m), axis=-1, keepdims=True)
            return (x - m) * jax.lax.rsqrt(v + LN_EPS) * w + b

        def modulate(x, shift, scale):
            return x * (1.0 + scale[:, None, :]) + shift[:, None, :]

        def attention(x, wq, wk, wv, wo, wo_b):
            b, s, d = x.shape
            q = (x @ wq).reshape(b, s, H, HD).transpose(0, 2, 1, 3)
            k = (x @ wk).reshape(b, s, H, HD).transpose(0, 2, 1, 3)
            v = (x @ wv).reshape(b, s, H, HD).transpose(0, 2, 1, 3)
            scale = 1.0 / np.sqrt(HD).astype(np.float32)
            att = jnp.einsum('bhqd,bhkd->bhqk', q, k) * scale
            att = jax.nn.softmax(att, axis=-1)
            out = jnp.einsum('bhqk,bhkd->bhqd', att, v)
            out = out.transpose(0, 2, 1, 3).reshape(b, s, d)
            return out @ wo + wo_b
        key = jax.random.key(seed)
        ks = jax.random.split(key, 16)
        s = 0.02
        return {'x': jax.random.normal(ks[0], (B, S, D), jnp.float32), 'c': jax.random.normal(ks[1], (B, D), jnp.float32), 'ln1_w': jnp.ones((D,), jnp.float32), 'ln1_b': jnp.zeros((D,), jnp.float32), 'wq': jax.random.normal(ks[2], (D, D), jnp.float32) * s, 'wk': jax.random.normal(ks[3], (D, D), jnp.float32) * s, 'wv': jax.random.normal(ks[4], (D, D), jnp.float32) * s, 'wo': jax.random.normal(ks[5], (D, D), jnp.float32) * s, 'wo_b': jnp.zeros((D,), jnp.float32), 'ln2_w': jnp.ones((D,), jnp.float32), 'ln2_b': jnp.zeros((D,), jnp.float32), 'fc1_w': jax.random.normal(ks[6], (D, HID), jnp.float32) * s, 'fc1_b': jnp.zeros((HID,), jnp.float32), 'fc2_w': jax.random.normal(ks[7], (HID, D), jnp.float32) * s, 'fc2_b': jnp.zeros((D,), jnp.float32), 'ada_w': jax.random.normal(ks[8], (D, 6 * D), jnp.float32) * s, 'ada_b': jnp.zeros((6 * D,), jnp.float32)}
    _L1_cond_all = _L1_cond_setup()
    _L1_cond_in = {k: v for k, v in _L1_cond_all.items() if k in ('ln1_w', 'ln1_b', 'wq', 'wk', 'wv', 'wo', 'wo_b', 'ln2_w', 'ln2_b', 'fc1_w', 'fc1_b', 'fc2_w', 'fc2_b', 'ada_w', 'ada_b')}
    del _L1_cond_all
    return {'x': x, 'cond_1152': cond_1152, 'L0_cond_w_adaln': _L0_cond_in['w_adaln'], 'L0_cond_b_adaln': _L0_cond_in['b_adaln'], 'L0_cond_w_qkv': _L0_cond_in['w_qkv'], 'L0_cond_b_qkv': _L0_cond_in['b_qkv'], 'L0_cond_w_proj': _L0_cond_in['w_proj'], 'L0_cond_b_proj': _L0_cond_in['b_proj'], 'L0_cond_w_gate': _L0_cond_in['w_gate'], 'L0_cond_w1': _L0_cond_in['w1'], 'L0_cond_b1': _L0_cond_in['b1'], 'L0_cond_w2': _L0_cond_in['w2'], 'L0_cond_b2': _L0_cond_in['b2'], 'L1_cond_ln1_w': _L1_cond_in['ln1_w'], 'L1_cond_ln1_b': _L1_cond_in['ln1_b'], 'L1_cond_wq': _L1_cond_in['wq'], 'L1_cond_wk': _L1_cond_in['wk'], 'L1_cond_wv': _L1_cond_in['wv'], 'L1_cond_wo': _L1_cond_in['wo'], 'L1_cond_wo_b': _L1_cond_in['wo_b'], 'L1_cond_ln2_w': _L1_cond_in['ln2_w'], 'L1_cond_ln2_b': _L1_cond_in['ln2_b'], 'L1_cond_fc1_w': _L1_cond_in['fc1_w'], 'L1_cond_fc1_b': _L1_cond_in['fc1_b'], 'L1_cond_fc2_w': _L1_cond_in['fc2_w'], 'L1_cond_fc2_b': _L1_cond_in['fc2_b'], 'L1_cond_ada_w': _L1_cond_in['ada_w'], 'L1_cond_ada_b': _L1_cond_in['ada_b']}

def reference(x, cond_1152, L0_cond_w_adaln, L0_cond_b_adaln, L0_cond_w_qkv, L0_cond_b_qkv, L0_cond_w_proj, L0_cond_b_proj, L0_cond_w_gate, L0_cond_w1, L0_cond_b1, L0_cond_w2, L0_cond_b2, L1_cond_ln1_w, L1_cond_ln1_b, L1_cond_wq, L1_cond_wk, L1_cond_wv, L1_cond_wo, L1_cond_wo_b, L1_cond_ln2_w, L1_cond_ln2_b, L1_cond_fc1_w, L1_cond_fc1_b, L1_cond_fc2_w, L1_cond_fc2_b, L1_cond_ada_w, L1_cond_ada_b):
    import jax
    import jax.numpy as jnp

    def _L0_cond_ref(x, c, w_adaln, b_adaln, w_qkv, b_qkv, w_proj, b_proj, w_gate, w1, b1, w2, b2):
        import jax, jax.numpy as jnp
        import numpy as np
        NUM_HEADS = 16
        NUM_EXPERTS = 4
        TOP_K = 2
        LN_EPS = 1e-06

        def _ln(h):
            mu = jnp.mean(h, axis=-1, keepdims=True)
            var = jnp.var(h, axis=-1, keepdims=True)
            return (h - mu) * jax.lax.rsqrt(var + LN_EPS)

        def _modulate(h, shift, scale):
            return h * (1.0 + scale[:, None, :]) + shift[:, None, :]
        B, N, C = x.shape
        nh = NUM_HEADS
        hd = C // nh
        mod = jax.nn.silu(c) @ w_adaln + b_adaln
        sh_msa, sc_msa, g_msa, sh_mlp, sc_mlp, g_mlp = jnp.split(mod, 6, axis=-1)
        h = _modulate(_ln(x), sh_msa, sc_msa)
        qkv = (h @ w_qkv + b_qkv).reshape(B, N, 3, nh, hd).transpose(2, 0, 3, 1, 4)
        q, k, v = (qkv[0], qkv[1], qkv[2])
        attn = jax.nn.softmax(jnp.einsum('bhqd,bhkd->bhqk', q, k) * hd ** (-0.5), axis=-1)
        o = jnp.einsum('bhqk,bhkd->bhqd', attn, v).transpose(0, 2, 1, 3).reshape(B, N, C)
        o = o @ w_proj + b_proj
        x = x + g_msa[:, None, :] * o
        xn = _modulate(_ln(x), sh_mlp, sc_mlp)
        xf = xn.reshape(-1, C)
        gate_logits = xf @ w_gate
        topk_logits, topk_idx = jax.lax.top_k(gate_logits, TOP_K)
        gates = jax.nn.softmax(topk_logits, axis=-1)
        cw = jnp.sum(jax.nn.one_hot(topk_idx, NUM_EXPERTS, dtype=xf.dtype) * gates[..., None], axis=1)
        hmid = jax.nn.gelu(jnp.einsum('tc,ech->eth', xf, w1) + b1[:, None, :], approximate=True)
        eo = jnp.einsum('eth,ehc->etc', hmid, w2) + b2[:, None, :]
        moe = jnp.einsum('te,etc->tc', cw, eo).reshape(B, N, C)
        return x + g_mlp[:, None, :] * moe

    def _L1_cond_ref(x, c, ln1_w, ln1_b, wq, wk, wv, wo, wo_b, ln2_w, ln2_b, fc1_w, fc1_b, fc2_w, fc2_b, ada_w, ada_b):
        import jax, jax.numpy as jnp
        import numpy as np
        B, S, D = (8, 128, 144)
        H = 16
        HD = D // H
        HID = int(D * 4.0)
        LN_EPS = 1e-05

        def layer_norm(x, w, b):
            m = jnp.mean(x, axis=-1, keepdims=True)
            v = jnp.mean(jnp.square(x - m), axis=-1, keepdims=True)
            return (x - m) * jax.lax.rsqrt(v + LN_EPS) * w + b

        def modulate(x, shift, scale):
            return x * (1.0 + scale[:, None, :]) + shift[:, None, :]

        def attention(x, wq, wk, wv, wo, wo_b):
            b, s, d = x.shape
            q = (x @ wq).reshape(b, s, H, HD).transpose(0, 2, 1, 3)
            k = (x @ wk).reshape(b, s, H, HD).transpose(0, 2, 1, 3)
            v = (x @ wv).reshape(b, s, H, HD).transpose(0, 2, 1, 3)
            scale = 1.0 / np.sqrt(HD).astype(np.float32)
            att = jnp.einsum('bhqd,bhkd->bhqk', q, k) * scale
            att = jax.nn.softmax(att, axis=-1)
            out = jnp.einsum('bhqk,bhkd->bhqd', att, v)
            out = out.transpose(0, 2, 1, 3).reshape(b, s, d)
            return out @ wo + wo_b
        mod = jax.nn.silu(c) @ ada_w + ada_b
        sh_msa, sc_msa, g_msa, sh_mlp, sc_mlp, g_mlp = jnp.split(mod, 6, axis=1)
        h = modulate(layer_norm(x, ln1_w, ln1_b), sh_msa, sc_msa)
        x = x + g_msa[:, None, :] * attention(h, wq, wk, wv, wo, wo_b)
        h = modulate(layer_norm(x, ln2_w, ln2_b), sh_mlp, sc_mlp)
        h = jax.nn.gelu(h @ fc1_w + fc1_b, approximate=False) @ fc2_w + fc2_b
        x = x + g_mlp[:, None, :] * h
        return x
    x = _L0_cond_ref(x, cond_1152, L0_cond_w_adaln, L0_cond_b_adaln, L0_cond_w_qkv, L0_cond_b_qkv, L0_cond_w_proj, L0_cond_b_proj, L0_cond_w_gate, L0_cond_w1, L0_cond_b1, L0_cond_w2, L0_cond_b2)
    x = _L1_cond_ref(x, cond_1152, L1_cond_ln1_w, L1_cond_ln1_b, L1_cond_wq, L1_cond_wk, L1_cond_wv, L1_cond_wo, L1_cond_wo_b, L1_cond_ln2_w, L1_cond_ln2_b, L1_cond_fc1_w, L1_cond_fc1_b, L1_cond_fc2_w, L1_cond_fc2_b, L1_cond_ada_w, L1_cond_ada_b)
    return x

_drawn_inputs = setup_inputs


def setup_inputs(seed=0):
    import zlib

    import numpy as np

    out = dict(_drawn_inputs(seed))
    spreads = {'L0_cond_b_adaln': (0.0, 0.546),
     'L0_cond_b_qkv': (0.0, 0.8),
     'L0_cond_b_proj': (0.0, 0.452),
     'L0_cond_b1': (0.0, 0.8),
     'L0_cond_b2': (0.0, 0.688),
     'L1_cond_ln1_w': (1.0, 0.6),
     'L1_cond_ln1_b': (0.0, 0.8),
     'L1_cond_wo_b': (0.0, 0.441),
     'L1_cond_ln2_w': (1.0, 0.6),
     'L1_cond_ln2_b': (0.0, 0.8),
     'L1_cond_fc1_b': (0.0, 0.8),
     'L1_cond_fc2_b': (0.0, 0.499),
     'L1_cond_ada_b': (0.0, 0.547)}
    factors = {'L0_cond_w_adaln': 3.017,
     'L0_cond_w_qkv': 8.0,
     'L0_cond_w_proj': 8.0,
     'L0_cond_w_gate': 5.62,
     'L0_cond_w1': 7.28,
     'L0_cond_w2': 6.643,
     'L1_cond_wq': 8.0,
     'L1_cond_wk': 8.0,
     'L1_cond_wv': 8.0,
     'L1_cond_wo': 8.0,
     'L1_cond_fc1_w': 5.185,
     'L1_cond_fc2_w': 4.847}
    for name, (base, spread) in spreads.items():
        noise = np.random.default_rng([zlib.crc32(name.encode()), seed]).standard_normal(out[name].shape)
        drawn = base * np.exp(spread * noise) if base else spread * noise
        out[name] = jnp.asarray(drawn.astype(out[name].dtype))
    for name, factor in factors.items():
        out[name] = (out[name] * factor).astype(out[name].dtype)
    return out
```

```python
from contextlib import ExitStack

import concourse.bass as bass
from concourse import mybir

ALU = mybir.AluOpType
ACT = mybir.ActivationFunctionType
AX = mybir.AxisListType
F32 = mybir.dt.float32
F32R = mybir.dt.float32r
BF16 = mybir.dt.bfloat16

P = 128
BATCH, SEQ, C = 16, 128, 144
HEADS, HD = 16, 9
EXPERTS, HID = 4, 576
SCALE = HD ** -0.5
EPS = (1e-6, 1e-5)

CM = P
CR = C - CM
SLOT = 32
NS = P // SLOT
G = 4
NG = BATCH // G
GT = G * SEQ
QUADS = 4
HQ = HEADS // QUADS
LEAD = 6
PARTS = 3
SROWS = PARTS * PARTS * HD
MROWS = SROWS + 2
CT = HD * HEADS
ROWS8 = 8 * HEADS
VW = 32
MT0 = EXPERTS * HID // P
MT1 = 5
MSET = (0, 1, 3, 4)


def build(nc, x, cond, w_adaln, b_adaln, w_qkv, b_qkv, w_proj, b_proj, w_gate, w1, b1, w2, b2,
          ln1_w, ln1_b, wq, wk, wv, wo, wo_b, ln2_w, ln2_b, fc1_w, fc1_b, fc2_w, fc2_b,
          ada_w, ada_b, out):
    qk_dram = nc.dram_tensor("qk_scratch", [G, 2, PARTS, CT, SEQ], BF16).ap()
    gate_dram = nc.dram_tensor("gate_scratch", [2, 2, BATCH, C], F32).ap()

    with ExitStack() as ctx:
        def sb(name, shape, dt=F32):
            return ctx.enter_context(nc.sbuf_tensor(name, shape, dt))

        def sem(name):
            return ctx.enter_context(nc.semaphore(name))

        bank = [ctx.enter_context(nc.psum_tensor(f"bank{i}", [P, 512], F32)) for i in range(8)]
        MOD_BANK = (0, 3)
        S_BANK, ST_BANK, O_BANK, PREP, SMALL = (0, 1), (2, 3), (4, 5), bank[6], bank[7]

        xs = sb("xs", [P, BATCH * C])
        ident = sb("ident", [P, P])
        identb = sb("identb", [P, P], BF16)

        stats = sb("stats", [P, G, 6])
        msum, mdif, sq2, mean, vdif, vown = [sb(n, [P, G]) for n in
                                             "msum mdif sq2 mean vdif vown".split()]
        rstd = sb("rstd", [P, G])
        var_eps = sb("var_eps", [P, G])
        minus_half = sb("minus_half", [P, G])
        xn = sb("xn", [P, G, CM])
        xr = sb("xr", [P, G, NS, SLOT])
        h32 = sb("h32", [P, GT])
        hhi = sb("hhi", [P, GT], F32R)
        hlo = sb("hlo", [P, GT], F32R)
        r32 = sb("r32", [P, GT])
        hR = sb("hR", [P, GT], F32R)

        a_main = sb("a_main", [P, 4, BATCH])
        b_main = sb("b_main", [P, 4, BATCH])
        a_rest = sb("a_rest", [P, 4, BATCH])
        b_rest = sb("b_rest", [P, 4, BATCH])
        mask = sb("mask", [P, 2])
        lnm = sb("lnm", [P, 4])
        lnr = sb("lnr", [P, 4])
        c_nat = sb("c_nat", [BATCH, C + 1])
        c_tmp = sb("c_tmp", [BATCH, 3 * C])
        cT = sb("cT", [P, BATCH])
        cTr = sb("cTr", [CR + 1, BATCH])
        gates = sb("gates", [BATCH, 2, 2 * C])
        g_att = sb("g_att", [P, G, C])
        g_mlp = sb("g_mlp", [P, G, C])

        sq = [sb(f"sq{l}", [P, 3 * C]) for l in range(2)]
        sqr = [sb(f"sqr{l}", [P, 3 * C]) for l in range(2)]
        bw = sb("bw", [P, EXPERTS, C])
        bw_flat = bw[:, :, :].rearrange("p e c -> p (e c)")
        wp32, wr32 = bw_flat[:, 0:2 * C], bw_flat[:, 2 * C:]
        wqk_hi = [sb(f"wqk_hi{l}", [P, 2 * C], F32R) for l in range(2)]
        wqk_lo = [sb(f"wqk_lo{l}", [P, 2 * C], F32R) for l in range(2)]
        wqk_r = [sb(f"wqk_r{l}", [P, 2 * C], F32R) for l in range(2)]
        wv_r = [sb(f"wv_r{l}", [P, C], F32R) for l in range(2)]
        wo_m = [sb(f"wo_m{l}", [P, C]) for l in range(2)]
        wo_r = [sb(f"wo_r{l}", [CR + 1, C]) for l in range(2)]

        N0, N1 = EXPERTS * HID, HID
        w1_hi = sb("w1_hi", [P, N0], F32R)
        w1_lo = sb("w1_lo", [P, N0], F32R)
        w1_r = sb("w1_r", [P, N0], F32R)
        f1_hi = sb("f1_hi", [P, N1], F32R)
        f1_lo = sb("f1_lo", [P, N1], F32R)
        f1_r = sb("f1_r", [P, N1], F32R)
        sg = sb("sg", [P, EXPERTS])
        sgr = sb("sgr", [P, EXPERTS])
        wg_hi = sb("wg_hi", [P, EXPERTS], F32R)
        wg_lo = sb("wg_lo", [P, EXPERTS], F32R)
        wg_r = sb("wg_r", [P, EXPERTS], F32R)
        w2_sb = sb("w2_sb", [P, EXPERTS * MT1, C])
        f2_sb = sb("f2_sb", [P, MT1, C])
        b2_sb = sb("b2_sb", [P, EXPERTS, C])

        hid = sb("hid", [P, MT0 * GT])
        hid4 = sb("hid4", [P, GT])
        NA = 6 * C
        ada_m = [hid[:, (2 * l) * NA:(2 * l + 1) * NA] for l in range(2)]
        ada_r = [hid[0:CR + 1, (2 * l + 1) * NA:(2 * l + 2) * NA] for l in range(2)]
        o = 4 * NA
        s1 = hid[:, o:o + N0]
        s1r = hid[:, o + N0:o + 2 * N0]
        o += 2 * N0
        sf = hid[:, o:o + N1]
        sfr = hid[:, o + N1:o + 2 * N1]

        parts = sb("parts", [P, 3, PARTS, GT], BF16)
        resid = sb("resid", [P, GT])
        QA = sb("QA", [P, G, HEADS, SEQ], BF16)
        KA = sb("KA", [P, G, HEADS, SEQ], BF16)
        V = sb("V", [P, G, HEADS, VW])
        mx = sb("mx", [P, HEADS])
        mp = sb("mp", [P, 2, HEADS], BF16)
        mT = sb("mT", [2 * HEADS, SEQ], BF16)
        pr = sb("pr", [P, 2, 512])
        osb = sb("osb", [P, 512])
        rinv = sb("rinv", [P, HEADS])
        an = sb("an", [P, C + 1])
        aT = sb("aT", [P, SEQ])
        aTr = sb("aTr", [CR + 1, SEQ])
        tmp = sb("tmp", [P, C])

        lgT = sb("lgT", [EXPERTS, GT])
        lg = sb("lg", [P, G, EXPERTS])
        lmax = sb("lmax", [P, G])
        beat = sb("beat", [P, EXPERTS, G, EXPERTS])
        cnt = sb("cnt", [P, G, EXPERTS])
        sel = sb("sel", [P, G, EXPERTS])
        dl = sb("dl", [P, G, EXPERTS])
        ex = sb("ex", [P, G, EXPERTS])
        es = sb("es", [P, G, EXPERTS])
        den = sb("den", [P, G])
        rden = sb("rden", [P, G])
        cw = sb("cw", [P, G, EXPERTS])
        bw2 = sb("bw2", [P, 2, C])
        bias2 = sb("bias2", [P, 2, C])
        acc = sb("acc", [P, C])

        names = """ld_x0 ld_x ld_c ld_ada0 ld_ada1 ld_ln ld_qkv0 ld_qkv1 ld_wo ld_w1 ld_f1 ld_w2
            zeroed pooled silu cond_T cond_c mod_mm mod_done gate_c gate_st wsplit qk_weights split_s
            stats_s sums_s vars_s aggr_s rstd_s normed T_done h_main h_hi h_rest r_hi h_ready
            qk_mm part_a part_r part_b part_c scr_w v_mm v_ready
            s_mm max_s msplit mt_mm mt_c m_ld st_mm exp_s pv_mm o_ev o_T rinv_s an_s a_T a_c
            proj_mm att_t x_att g_att_ld g_mlp_ld gate_x cw_b mix_s mod_read
            gl_mm gl_c lg_T gate_s gate_e cw_s b2_s w1_mm gelu w2_mm acc_s acc_g x_mlp
            f1_mm f1_gelu f2_mm f2_t st_out""".split()
        s = {n: sem(n) for n in names}
        qk_ld = [sem(f"qk_ld{j}") for j in range(G)]

        def need(eng, name, value):
            if isinstance(value, int) and value <= 0:
                return
            eng.wait_ge(s[name], value)

        def xt(t):
            return xs[:, bass.ds(t * C, C)] if not isinstance(t, int) else xs[:, t * C:(t + 1) * C]

        def col(tile, ph, t):
            return tile[:, ph, t:t + 1] if isinstance(t, int) else tile[:, ph, bass.ds(t, 1)]

        def following(ph, g):
            if isinstance(g, int) and g == NG - 1:
                return (ph + 1, 0) if ph < 3 else None
            return ph, g + 1

        def attention_order(first, last):
            for k in range(G if not last else G + 2):
                for q in range(QUADS):
                    pos = QUADS * k + q
                    own = k < G
                    if pos == 0:
                        yield "NORM", 1
                    if pos + LEAD < QUADS * G or (own and not last):
                        yield "MAX", pos + LEAD
                    if own:
                        yield "SCORE", pos
                    if pos - 1 < QUADS * G and not (first and pos == 0):
                        yield "PV", pos - 1
                    if q == 0 and k - 2 < G and not (first and k < 2):
                        yield "PROJ", k - 2
                    if pos == 0:
                        yield "V", (0, 1)
                    if q == 1 and k - 1 < G and not (first and k < 1):
                        yield "OUT_T", k - 1
                    if q == 2 and (k + 1 < G or (own and not last)):
                        yield "MAX_T", k + 1
                    if q == 3 and k - 1 < G and not (first and k < 1):
                        yield "ATT_T", k - 1
                    if pos == 2:
                        yield "H_MAIN", 1
                    if pos == 3:
                        yield "H_REST", 1
                    if pos == 5:
                        yield "GATE_LOAD", 0
                    if own and not last:
                        if pos in (5, 6, 7):
                            yield "QK", pos - 5
                        if pos in (6, 7, 8):
                            yield "QK_PARTS", pos - 6
                        if pos == 8:
                            yield "LOAD", 0
                            yield "LOAD", 1
                        if pos == 12:
                            yield "LOAD", 2
                        if pos == 14:
                            yield "V", (1, 0)
                        if pos == 15:
                            yield "LOAD", 3

        def attention_start():
            for t in range(3):
                yield "QK", t
                yield "QK_PARTS", t
            yield "V", (0, 0)
            for j in range(G):
                yield "LOAD", j
            for p in range(LEAD):
                yield "MAX", p
                if p == 3:
                    yield "MAX_T", 0

        def mlp_order(L, more):
            yield "GATE_LOAD", 0
            if more:
                yield "NORM", 1
            if L == 0:
                yield "LOGITS", 0
            for m in range(MT0 if L == 0 else MT1):
                yield "UP", m
                if L == 0 and m == 3:
                    yield "LOGITS_T", 0
                if L == 0 and m == 8:
                    yield "MIX", 0
            yield "DOWN", 0
            if more:
                yield "H_MAIN", 1
            yield "DOWN", 1
            if more:
                yield "H_REST", 1
            yield "DOWN", 2
            yield "DOWN", 3

        def phases(eng, setup, attention, mlp):
            def group(order, stage, L, g):
                for what, i in order:
                    stage(what, i, L, g)

            setup()
            for L in range(2):
                for what, i in attention_start():
                    attention(what, i, L, 0, True)
                group(attention_order(True, False), attention, L, 0)
                with eng.Fori(1, NG - 1) as g:
                    group(attention_order(False, False), attention, L, g)
                group(attention_order(False, True), attention, L, NG - 1)
                group(mlp_order(L, True), mlp, L, 0)
                with eng.Fori(1, NG - 1) as g:
                    group(mlp_order(L, True), mlp, L, g)
                group(mlp_order(L, L == 0), mlp, L, NG - 1)

        def after(ph, g):
            return (ph + 1, 0) if isinstance(g, int) and g == NG - 1 else (ph, g + 1)

        def inputs_used(eng, ph, g):
            if isinstance(g, int) and g == 0:
                ph, g = ph - 1, NG
            if ph in (0, 2):
                need(eng, "v_mm", 2 * (NG * (ph // 2) + g))
            elif ph > 0:
                need(eng, *(("w1_mm", MT0 * g) if ph == 1 else ("f1_mm", MT1 * g)))

        def rows(t):
            return P if t < 2 else 2 * HEADS

        NADA = 16 * 3
        NW2 = 16 * (2 * EXPERTS + 4)
        NLN = 16 * (4 + 4 * NS)
        NQKV = (16 * (1 + 2 * NS), 16 * (3 + 3 * NS))
        block = ctx.enter_context(nc.Block())

        @block.sync
        def _(sp):
            xv = x.rearrange("b p c -> p b c")
            xd = xs[:, :].rearrange("p (b c) -> p b c", c=C)
            sp.dma_start(c_nat[:, 0:C], cond).then_inc(s["ld_c"], 16)
            sp.dma_start(xd[:, 0:G], xv[:, 0:G]).then_inc(s["ld_x0"], 16)

            def load_ada(L, w, b):
                done = s[f"ld_ada{L}"]
                sp.dma_start(ada_m[L], w[0:CM, :]).then_inc(done, 16)
                sp.dma_start(ada_r[L][0:CR, :], w[CM:C, :]).then_inc(done, 16)
                sp.dma_start(ada_r[L][CR:CR + 1, :], b.unsqueeze(0)).then_inc(done, 16)

            load_ada(0, w_adaln, b_adaln)
            sp.dma_start(sq[0][:, :], w_qkv[0:CM, :]).then_inc(s["ld_qkv0"], 16)
            need(sp, "zeroed", 1)
            for k in range(NS):
                sp.dma_start(sqr[0][SLOT * k:SLOT * k + CR, :], w_qkv[CM:C, :]).then_inc(s["ld_qkv0"], 16)
                sp.dma_start(sqr[0][SLOT * k + CR:SLOT * k + CR + 1, :],
                             b_qkv.unsqueeze(0)).then_inc(s["ld_qkv0"], 16)
            load_ada(1, ada_w, ada_b)
            need(sp, "pooled", 1)
            for i, v in enumerate((ln1_w, ln1_b, ln2_w, ln2_b)):
                sp.dma_start(lnm[:, i:i + 1], v[0:CM].unsqueeze(1)).then_inc(s["ld_ln"], 16)
                for k in range(NS):
                    sp.dma_start(lnr[SLOT * k:SLOT * k + CR, i:i + 1],
                                 v[CM:C].unsqueeze(1)).then_inc(s["ld_ln"], 16)
            sp.dma_start(xd[:, G:], xv[:, G:]).then_inc(s["ld_x"], 16)
            for L, (w, b) in enumerate(((w_proj, b_proj), (wo, wo_b))):
                sp.dma_start(wo_m[L][:, :], w[0:CM, :]).then_inc(s["ld_wo"], 16)
                sp.dma_start(wo_r[L][0:CR, :], w[CM:C, :]).then_inc(s["ld_wo"], 16)
                sp.dma_start(wo_r[L][CR:CR + 1, :], b.unsqueeze(0)).then_inc(s["ld_wo"], 16)

            def load_late():
                for i, w in enumerate((wq, wk, wv)):
                    sp.dma_start(sq[1][:, i * C:(i + 1) * C], w[0:CM, :]).then_inc(s["ld_qkv1"], 16)
                    for k in range(NS):
                        sp.dma_start(sqr[1][SLOT * k:SLOT * k + CR, i * C:(i + 1) * C],
                                     w[CM:C, :]).then_inc(s["ld_qkv1"], 16)
                e = w1.rearrange("e c h -> c e h")
                sp.dma_start(s1.rearrange("p (e h) -> p e h", e=EXPERTS), e[0:CM]).then_inc(s["ld_w1"], 16)
                sp.dma_start(sg[:, :], w_gate[0:CM, :]).then_inc(s["ld_w1"], 16)
                sp.dma_start(sf, fc1_w[0:CM, :]).then_inc(s["ld_f1"], 16)
                need(sp, "zeroed", 2)
                need(sp, "pooled", 4)
                b1f = b1.rearrange("e h -> (e h)").unsqueeze(0)
                for k in range(NS):
                    a = SLOT * k
                    sp.dma_start(s1r[a:a + CR, :].rearrange("p (e h) -> p e h", e=EXPERTS),
                                 e[CM:C]).then_inc(s["ld_w1"], 16)
                    sp.dma_start(s1r[a + CR:a + CR + 1, :], b1f).then_inc(s["ld_w1"], 16)
                    sp.dma_start(sgr[a:a + CR, :], w_gate[CM:C, :]).then_inc(s["ld_w1"], 16)
                    sp.dma_start(sfr[a:a + CR, :], fc1_w[CM:C, :]).then_inc(s["ld_f1"], 16)
                    sp.dma_start(sfr[a + CR:a + CR + 1, :], fc1_b.unsqueeze(0)).then_inc(s["ld_f1"], 16)
                half = P // 2
                for e in range(EXPERTS):
                    m, odd = MT1 * e, e % 2
                    sp.dma_start(w2_sb[:, m + odd:m + odd + 4, :],
                                 w2[e, odd * half:odd * half + 4 * P, :].rearrange("(m p) c -> p m c", p=P)
                                 ).then_inc(s["ld_w2"], 16)
                    if odd:
                        sp.dma_start(w2_sb[half:P, m, :], w2[e, 0:half, :]).then_inc(s["ld_w2"], 16)
                    else:
                        sp.dma_start(w2_sb[0:half, m + 4, :], w2[e, 4 * P:HID, :]).then_inc(s["ld_w2"], 16)
                sp.dma_start(b2_sb[:, :, :], b2.partition_broadcast(P)).then_inc(s["ld_w2"], 16)
                sp.dma_start(f2_sb[:, 0:4, :],
                             fc2_w[0:4 * P, :].rearrange("(m p) c -> p m c", p=P)).then_inc(s["ld_w2"], 16)
                sp.dma_start(f2_sb[0:HID - 4 * P, 4, :], fc2_w[4 * P:HID, :]).then_inc(s["ld_w2"], 16)
                sp.dma_start(f2_sb[HID - 4 * P:HID - 4 * P + 1, 4, :],
                             fc2_b.unsqueeze(0)).then_inc(s["ld_w2"], 16)

            def store_parts(a, t):
                if t == 0:
                    need(sp, "s_mm", 16 * (a - 1) + 13)
                need(sp, "part_c", 3 * a + t + 1)
                for which, lo, n, row in (((t, 0, ROWS8, 0),) if t < 2 else
                                          ((0, 0, HEADS, ROWS8), (1, HEADS, HEADS, ROWS8))):
                    for p in range(PARTS):
                        sp.dma_start(qk_dram[:, which, p, row:row + n, :].rearrange("j c t -> c j t"),
                                     parts[lo:lo + n, t, p, :].rearrange("c (j t) -> c j t", j=G)
                                     ).then_inc(s["scr_w"], 16)

            def load_qk(a, j):
                slot_free = 16 * a - 16 + 4 * j + 4
                if not isinstance(a, int):
                    slot_free = sp.snap(slot_free)
                need(sp, "st_mm", slot_free)
                if j == 0:
                    need(sp, "scr_w", 192 * (a + 1))
                for p in range(PARTS):
                    r = p * PARTS * HD
                    sp.dma_start(QA[r:r + PARTS * HD, j, :, :].rearrange("p h t -> p (h t)"),
                                 qk_dram[j, 0].rearrange("s (d h) t -> (s d) (h t)", h=HEADS)
                                 ).then_inc(qk_ld[j], 16)
                    sp.dma_start(KA[r:r + PARTS * HD, j, :, :].rearrange("p h t -> p (h t)"),
                                 qk_dram[j, 1, p].rearrange("(d h) t -> d (h t)", h=HEADS)
                                 .partition_broadcast(PARTS)).then_inc(qk_ld[j], 16)

            def put_max(B, j):
                need(sp, "mt_c", B + 1)
                sp.dma_start(QA[SROWS:MROWS, j, :, :], mT[:, :]).then_inc(s["m_ld"], 16)

            def load_gate(L, which, g, dst, name, done, count):
                need(sp, done, count)
                src = gate_dram[L, which, bass.ds(G * g, G), :] if not isinstance(g, int) \
                    else gate_dram[L, which, G * g:G * (g + 1), :]
                sp.dma_start(dst[:, :, :], src.partition_broadcast(P)).then_inc(s[name], 16)

            def setup():
                load_late()

            def attention(what, i, L, g, start=False):
                a = NG * L + g
                if what == "GATE_LOAD":
                    load_gate(L, 0, g, g_att, "g_att_ld", "x_att", G * a)
                if what == "MAX_T":
                    put_max(G * a + i, i % G)
                if start and what == "MAX" and i == LEAD - 1 and L == 0:
                    for l in range(2):
                        need(sp, "gate_c", 2 * l + 2)
                        sp.dma_start(gate_dram[l].rearrange("w b c -> b w c"),
                                     gates[:, l, :].rearrange("b (w c) -> b w c", w=2)
                                     ).then_inc(s["gate_st"], 16)
                    need(sp, "gate_st", 32)
                nxt = a if start else a + 1
                if what == "QK_PARTS":
                    store_parts(nxt, i)
                if what == "LOAD":
                    load_qk(nxt, i)

            def mlp(what, i, L, g):
                m = NG * L + g
                if what == "GATE_LOAD":
                    load_gate(L, 1, g, g_mlp, "g_mlp_ld", "x_mlp", G * m)
                if what == "DOWN" and i == G - 1 and L == 1:
                    need(sp, "x_mlp", G * m + G)
                    t = G * g
                    ov = out.rearrange("b p c -> p b c")
                    dst = ov[:, t:t + G, :] if isinstance(g, int) else ov[:, bass.ds(t, G), :]
                    src = xs[:, t * C:(t + G) * C] if isinstance(g, int) \
                        else xs[:, bass.ds(t * C, G * C)]
                    sp.dma_start(dst, src.rearrange("p (b c) -> p b c", c=C)).then_inc(s["st_out"], 16)

            phases(sp, setup, attention, mlp)
            sp.wait_ge(s["st_out"], 16 * NG)

        @block.gpsimd
        def _(pool):
            gp = nc.gpsimd
            gp.memset(ident[:, :], 0.0)
            gp.memset(identb[:, :], 0.0)
            gp.memset(xr[:, :, :, :], 0.0)
            gp.memset(minus_half[:, :], -0.5)
            gp.memset(lnr[:, 0:1], 1.0)
            gp.memset(lnr[:, 1:2], 0.0)
            gp.memset(lnr[:, 2:3], 1.0)
            gp.memset(lnr[:, 3:4], 0.0).then_inc(s["pooled"], 1)
            pool.wait_ge(s["pooled"], 1)
            for m in (ident, identb):
                gp.affine_select(out=m[:, :], in_=m[:, :], compare_op=ALU.not_equal, fill=1.0, base=0,
                                 pattern=[[-1, P]], channel_multiplier=1)
            gp.memset(xr[:, :, :, CR:CR + 1], 1.0).then_inc(s["pooled"], 1)
            gp.memset(V[:, :, :, :], 0.0).then_inc(s["pooled"], 1)
            pool.wait_ge(s["pooled"], 3)
            gp.memset(V[:, :, :, HD:HD + 1], 1.0)
            gp.memset(sgr[:, :], 0.0)
            gp.memset(beat[:, :, :, :], 0.0)
            gp.memset(an[:, C:C + 1], 1.0).then_inc(s["pooled"], 1)

            def split(n, hi, lo, rest, src, srcr):
                gp.tensor_tensor(lo[:, :], src, hi[:, :].bitcast(F32),
                                 ALU.subtract).then_inc(s["split_s"], 1)
                pool.wait_ge(s["split_s"], 3 * n + 1)
                for i in range(2):
                    a = SLOT * (2 * i + 1)
                    gp.tensor_tensor(rest[a:a + SLOT, :], srcr[a:a + SLOT, :],
                                     rest[a:a + SLOT, :].bitcast(F32),
                                     ALU.subtract).then_inc(s["split_s"], 1)
                    pool.wait_ge(s["split_s"], 3 * n + 2 + i)

            def inverse_deviation(ph, g):
                n = NG * ph + g
                need(pool, "aggr_s", n + 1)
                gp.tensor_tensor(rstd[:, :], var_eps[:, :], minus_half[:, :],
                                 ALU.pow).then_inc(s["rstd_s"], 1)

            def part_c(a, t):
                n = rows(t)
                need(pool, "part_b", 3 * a + t + 1)
                gp.tensor_tensor(parts[0:n, t, 2, :], resid[0:n, :], parts[0:n, t, 1, :],
                                 ALU.subtract).then_inc(s["part_c"], 1)

            def attention(what, i, L, g, start=False):
                a = NG * L + g
                if what == "NORM":
                    inverse_deviation(*after(2 * L, g))
                if what == "QK_PARTS":
                    part_c(a if start else a + 1, i)
                if L == 0 and not start and isinstance(g, int):
                    if g == 0 and what == "QK_PARTS" and i == 2:
                        pool.wait_ge(s["wsplit"], 1)
                        split(0, w1_hi, w1_lo, w1_r, s1, s1r)
                    if g == NG - 1 and what == "GATE_LOAD":
                        pool.wait_ge(s["wsplit"], 2)
                        split(1, wg_hi, wg_lo, wg_r, sg[:, :], sgr[:, :])
                        split(2, f1_hi, f1_lo, f1_r, sf, sfr)

            def mlp(what, i, L, g):
                if what == "NORM":
                    inverse_deviation(*after(2 * L + 1, g))
                if what != "MIX":
                    return
                if isinstance(g, int) and g == 0:
                    pool.wait_ge(s["ld_w2"], NW2)
                for j in range(G):
                    t = G * g + j
                    if j == 0:
                        need(pool, "cw_s", g + 1)
                    wcol = cw[:, j, :].unsqueeze(2).to_broadcast([P, EXPERTS, C])
                    need(pool, "b2_s", 3 * t - 1)
                    gp.tensor_tensor(bw[:, :, :], b2_sb[:, :, :], wcol, ALU.mult).then_inc(s["b2_s"], 1)
                    need(pool, "b2_s", 3 * t + 1)
                    gp.tensor_tensor(bw2[:, :, :], bw[:, 0:2, :], bw[:, 2:4, :],
                                     ALU.add).then_inc(s["b2_s"], 1)
                    need(pool, "b2_s", 3 * t + 2)
                    need(pool, "acc_s", 4 * (t - 2) + 1)
                    gp.tensor_tensor(bias2[:, j % 2, :], bw2[:, 0, :], bw2[:, 1, :],
                                     ALU.add).then_inc(s["b2_s"], 1)

            phases(pool, lambda: inverse_deviation(0, 0), attention, mlp)

        @block.scalar
        def _(act):
            sc = nc.scalar

            def h_main(ph, g):
                n = NG * ph + g
                inputs_used(act, ph, g)
                if isinstance(n, int) and n == 0:
                    act.wait_ge(s["mod_read"], 1)
                need(act, "T_done", 2 * n + 1)
                for j in range(G):
                    t = G * g + j
                    last = sc.activation(h32[:, j * SEQ:(j + 1) * SEQ], PREP[:, j * SEQ:(j + 1) * SEQ],
                                         ACT.Identity, bias=col(b_main, ph, t), scale=col(a_main, ph, t))
                last.then_inc(s["h_main"], 1)

            def part_a(a, t):
                n = P if t < 2 else 2 * HEADS
                if t == 0:
                    need(act, "scr_w", 192 * a)
                need(act, "qk_mm", 3 * a + t + 1)
                sc.copy(parts[0:n, t, 0, :], PREP[0:n, :]).then_inc(s["part_a"], 1)

            def part_b(a, t):
                n = P if t < 2 else 2 * HEADS
                need(act, "part_r", 3 * a + t + 1)
                sc.copy(parts[0:n, t, 1, :], resid[0:n, :]).then_inc(s["part_b"], 1)

            def v_out(a, k):
                need(act, "v_mm", 2 * a + k + 1)
                need(act, "pv_mm", 16 * (a - 1) + (12 if k == 0 else 16))
                if isinstance(a, int) and a == 0 and k == 0:
                    act.wait_ge(s["pooled"], 4)
                j0, n = ((0, 3), (3, 1))[k]
                sc.copy(V[:, j0:j0 + n, :, 0:HD].rearrange("p j h d -> p (j h) d"),
                        PREP[:, 0:n * C].rearrange("p (h d) -> p h d", d=HD)).then_inc(s["v_ready"], 1)

            def m_out(B):
                need(act, "mt_mm", B + 1)
                need(act, "m_ld", 16 * B)
                sc.copy(mT[:, :], SMALL[0:2 * HEADS, 0:SEQ // 2].bitcast(BF16)).then_inc(s["mt_c"], 1)

            def exp_quad(qi, q):
                need(act, "st_mm", qi + 1)
                need(act, "pv_mm", qi - 1)
                sc.activation(pr[:, q % 2, :], bank[ST_BANK[q % 2]][:, :], ACT.Exp,
                              scale=SCALE).then_inc(s["exp_s"], 1)

            def o_out(B, j):
                need(act, "pv_mm", 4 * B + 4)
                need(act, "o_T", B)
                sc.copy(osb[:, :], bank[O_BANK[j % 2]][:, :]).then_inc(s["o_ev"], 1)

            def a_out(B):
                need(act, "a_T", B + 1)
                need(act, "proj_mm", B)
                sc.copy(aT[:, :], SMALL[:, 0:SEQ])
                sc.copy(aTr[:, :], SMALL[0:CR + 1, SEQ:2 * SEQ]).then_inc(s["a_c"], 1)

            def gates_out(L):
                act.wait_ge(s["mod_mm"], 3 * L + 3)
                for w in range(2):
                    sc.copy(gates[:, L, w * C:(w + 1) * C],
                            bank[O_BANK[L]][0:BATCH, w * C:(w + 1) * C]).then_inc(s["gate_c"], 1)

            def setup():
                act.wait_ge(s["ld_c"], 16)
                sc.activation(c_tmp[:, C:2 * C], c_nat[:, 0:C], ACT.Exp, scale=-1.0).then_inc(s["silu"], 1)
                act.wait_ge(s["cond_T"], 1)
                sc.copy(cT[:, :], SMALL[:, 0:BATCH])
                sc.copy(cTr[:, :], SMALL[0:CR + 1, BATCH:2 * BATCH]).then_inc(s["cond_c"], 1)
                gates_out(0)

            def attention(what, i, L, g, start=False):
                a = NG * L + g
                nxt = a if start else a + 1
                if what == "SCORE":
                    exp_quad(16 * a + i, i % 2)
                if what == "PV" and i % QUADS == QUADS - 1:
                    o_out(G * a + i // QUADS, i // QUADS)
                if what == "MAX_T":
                    m_out(G * a + i)
                if what == "ATT_T":
                    a_out(G * a + i)
                if what == "V":
                    v_out(a + i[0] if not start else a, i[1])
                if what == "H_MAIN":
                    h_main(*after(2 * L, g))
                if what == "QK":
                    part_a(nxt, i)
                if what == "QK_PARTS":
                    part_b(nxt, i)
                if start and what == "MAX" and i == LEAD - 1 and L == 0:
                    gates_out(1)
                if L == 0 and not start and isinstance(g, int):
                    if g == 0 and what == "QK_PARTS" and i == 2:
                        act.wait_ge(s["ld_w1"], 16 * (2 + 3 * NS))
                        sc.copy(w1_hi[:, :], s1)
                        sc.copy(w1_r[:, :], s1r).then_inc(s["wsplit"], 1)
                    if g == NG - 1 and what == "GATE_LOAD":
                        act.wait_ge(s["ld_f1"], 16 * (1 + 2 * NS))
                        for dst, src in ((wg_hi[:, :], sg[:, :]), (wg_r[:, :], sgr[:, :]),
                                         (f1_hi[:, :], sf), (f1_r[:, :], sfr)):
                            last = sc.copy(dst, src)
                        last.then_inc(s["wsplit"], 1)

            def mlp(what, i, L, g):
                if what == "LOGITS":
                    need(act, "gl_mm", g + 1)
                    need(act, "lg_T", g)
                    sc.copy(lgT[:, :], SMALL[0:EXPERTS, :]).then_inc(s["gl_c"], 1)
                if what == "UP" and L == 0:
                    if i == 0 and isinstance(g, int) and g == 0:
                        act.wait_ge(s["split_s"], 9)
                    if i == 0:
                        need(act, "w2_mm", 8 * g)
                    need(act, "w1_mm", MT0 * g + i + 1)
                    sc.activation(hid[:, i * GT:(i + 1) * GT], bank[i % 4][:, :],
                                  ACT.Gelu_apprx_tanh).then_inc(s["gelu"], 1)
                if what == "UP" and L == 1:
                    if i == 0:
                        need(act, "w2_mm", 8 * NG)
                        need(act, "f2_mm", G * g)
                    need(act, "f1_mm", MT1 * g + i + 1)
                    n = P if i < 4 else HID - 4 * P
                    dst = hid[:, i * GT:(i + 1) * GT] if i < 4 else hid4[0:n, :]
                    sc.activation(dst, bank[i % 4][0:n, :], ACT.Gelu).then_inc(s["f1_gelu"], 1)
                if what == "MIX":
                    need(act, "gate_e", g + 1)
                    sc.activation(ex[:, :, :], dl[:, :, :], ACT.Exp).then_inc(s["gate_x"], 1)
                if what == "H_MAIN":
                    h_main(*after(2 * L + 1, g))

            def start():
                setup()
                h_main(0, 0)

            phases(act, start, attention, mlp)

        @block.vector
        def _(dve):
            v = nc.vector
            done = [0]

            def step(ins):
                done[0] += 1
                ins.then_inc(s["mod_done"], 1)
                dve.wait_ge(s["mod_done"], done[0])

            def weights(L):
                dve.wait_ge(s["ld_qkv%d" % L], NQKV[L])
                for src, dst in ((sq[L], wp32), (sqr[L], wr32)):
                    sv = src[:, 0:2 * C].rearrange("p (w h d) -> p w d h", w=2, d=HD)
                    for w in range(2):
                        v.tensor_copy(dst[:, w * ROWS8:(w + 1) * ROWS8].rearrange("p (d h) -> p d h", d=8),
                                      sv[:, w, 0:8, :])
                    last = v.tensor_copy(dst[:, 2 * ROWS8:2 * C].rearrange("p (w h) -> p w h", w=2),
                                         sv[:, :, 8, :])
                step(last)
                v.tensor_copy(wqk_hi[L][:, :], wp32[:, :])
                v.tensor_copy(wqk_r[L][:, :], wr32[:, :])
                step(v.tensor_copy(wv_r[L][:, :], sqr[L][:, 2 * C:3 * C]))
                v.tensor_tensor(wqk_lo[L][:, :], wp32[:, :], wqk_hi[L][:, :].bitcast(F32), ALU.subtract)
                for k in (1, 3):
                    a, b = SLOT * k, SLOT * (k + 1)
                    v.tensor_tensor(wqk_r[L][a:b, :], wr32[a:b, :], wqk_r[L][a:b, :].bitcast(F32),
                                    ALU.subtract)
                    last = v.tensor_tensor(wv_r[L][a:b, :], sqr[L][a:b, 2 * C:3 * C],
                                           wv_r[L][a:b, :].bitcast(F32), ALU.subtract)
                last.then_inc(s["qk_weights"], 1)
                dve.wait_ge(s["qk_weights"], L + 1)

            def modulation(L):
                dve.wait_ge(s["mod_mm"], 3 * L + 1)
                if L == 1:
                    dve.wait_ge(s["ld_ln"], NLN)
                bk = bank[MOD_BANK[L]]
                for i in range(2):
                    ph = 2 * L + i
                    sh, scl = bk[:, 32 * i:32 * i + 16], bk[:, 32 * i + 16:32 * i + 32]
                    shr, sclr = bk[:, 64 + 32 * i:80 + 32 * i], bk[:, 80 + 32 * i:96 + 32 * i]
                    v.tensor_scalar(a_main[:, ph, :], scl, 1.0, None, ALU.add)
                    v.tensor_copy(b_main[:, ph, :], sh)
                    v.tensor_scalar(a_rest[:, ph, :], sclr, mask[:, 0:1], mask[:, 1:2], ALU.mult, ALU.add)
                    step(v.tensor_scalar(b_rest[:, ph, :], shr, mask[:, 0:1], None, ALU.mult))
                    if L == 1:
                        for a, b, ln in ((a_main, b_main, lnm), (a_rest, b_rest, lnr)):
                            step(v.scalar_tensor_tensor(b[:, ph, :], a[:, ph, :], ln[:, 2 * i + 1:2 * i + 2],
                                                        b[:, ph, :], ALU.mult, ALU.add))
                            step(v.tensor_scalar(a[:, ph, :], a[:, ph, :], ln[:, 2 * i:2 * i + 1], None,
                                                 ALU.mult))
                v.tensor_copy(c_tmp[:, 0:1], c_tmp[:, C:C + 1]).then_inc(s["mod_read"], 1)

            def norm(ph, g):
                n = NG * ph + g
                if ph == 0:
                    if isinstance(g, int) and g == 0:
                        dve.wait_ge(s["ld_x0"], 16)
                    else:
                        dve.wait_ge(s["ld_x"], 16)
                elif ph == 2:
                    need(dve, "x_mlp", G * g + G)
                else:
                    need(dve, "x_att", BATCH * (ph // 2) + G * g + G)
                need(dve, "normed", n)
                for j in range(G):
                    last = v.bn_stats(stats[:, j, :], xt(G * g + j))
                last.then_inc(s["stats_s"], 1)
                need(dve, "stats_s", n + 1)
                even, odd = stats[:, :, 0:3], stats[:, :, 3:6]
                v.tensor_tensor(msum[:, :], even[:, :, 1], odd[:, :, 1], ALU.add)
                v.tensor_tensor(mdif[:, :], even[:, :, 1], odd[:, :, 1], ALU.subtract)
                v.tensor_tensor(sq2[:, :], even[:, :, 2], odd[:, :, 2], ALU.add).then_inc(s["sums_s"], 1)
                need(dve, "sums_s", n + 1)
                v.tensor_scalar(mean[:, :], msum[:, :], 0.5, None, ALU.mult)
                v.scalar_tensor_tensor(vdif[:, :], mdif[:, :], 0.25, mdif[:, :], ALU.mult, ALU.mult)
                v.tensor_scalar(vown[:, :], sq2[:, :], 1.0 / C, EPS[ph // 2], ALU.mult,
                                ALU.add).then_inc(s["vars_s"], 1)
                need(dve, "vars_s", n + 1)
                v.tensor_tensor(var_eps[:, :], vdif[:, :], vown[:, :], ALU.add).then_inc(s["aggr_s"], 1)
                need(dve, "rstd_s", n + 1)
                need(dve, "T_done", 2 * n)
                if isinstance(n, int) and n == 0:
                    dve.wait_ge(s["pooled"], 2)
                for j in range(G):
                    x_ = xt(G * g + j)
                    v.tensor_scalar(xn[:, j, :], x_[:, 0:CM], mean[:, j:j + 1], rstd[:, j:j + 1],
                                    ALU.subtract, ALU.mult)
                    last = v.tensor_scalar(xr[:, j, :, 0:CR],
                                           x_[:, CM:C].unsqueeze(1).to_broadcast([P, NS, CR]),
                                           mean[:, j:j + 1], rstd[:, j:j + 1], ALU.subtract, ALU.mult)
                last.then_inc(s["normed"], 1)

            def h_rest(ph, g):
                n = NG * ph + g
                need(dve, "T_done", 2 * n + 2)
                inputs_used(dve, ph, g)
                for j in range(G):
                    t = G * g + j
                    last = v.tensor_scalar(r32[:, j * SEQ:(j + 1) * SEQ], PREP[:, j * SEQ:(j + 1) * SEQ],
                                           col(a_rest, ph, t), col(b_rest, ph, t), ALU.mult, ALU.add)
                last.then_inc(s["h_rest"], 1)
                need(dve, "h_main", n + 1)
                v.tensor_copy(hhi[:, :], h32[:, :]).then_inc(s["h_hi"], 1)
                need(dve, "h_rest", n + 1)
                v.tensor_copy(hR[:, :], r32[:, :]).then_inc(s["r_hi"], 1)
                need(dve, "h_hi", n + 1)
                v.tensor_tensor(hlo[:, :], h32[:, :], hhi[:, :].bitcast(F32), ALU.subtract)
                need(dve, "r_hi", n + 1)
                half = slice(2 * SLOT, P)
                v.tensor_tensor(hR[half, :], r32[half, :], hR[half, :].bitcast(F32),
                                ALU.subtract).then_inc(s["h_ready"], 1)

            def part_r(a, t):
                n = P if t < 2 else 2 * HEADS
                need(dve, "part_a", 3 * a + t + 1)
                need(dve, "part_c", 3 * a + t)
                v.tensor_tensor(resid[0:n, :], PREP[0:n, :], parts[0:n, t, 0, :],
                                ALU.subtract).then_inc(s["part_r"], 1)

            def row_max(B, q):
                need(dve, "s_mm", 4 * B + q + 1)
                if q == 0:
                    need(dve, "msplit", 2 * B)
                v.tensor_reduce(mx[:, HQ * q:HQ * (q + 1)],
                                bank[S_BANK[q % 2]][:, :].rearrange("p (h k) -> p h k", k=SEQ),
                                AX.X, ALU.max).then_inc(s["max_s"], 1)

            def max_split(B):
                need(dve, "max_s", 4 * B + 4)
                need(dve, "mt_mm", B)
                v.tensor_copy(mp[:, 0, :], mx[:, :]).then_inc(s["msplit"], 1)
                need(dve, "msplit", 2 * B + 1)
                v.tensor_tensor(mp[:, 1, :], mx[:, :], mp[:, 0, :], ALU.subtract).then_inc(s["msplit"], 1)
                need(dve, "msplit", 2 * B + 2)

            def normalise(B):
                need(dve, "o_T", B + 1)
                ov = SMALL[:, :].rearrange("p (h w) -> p h w", w=VW)
                v.reciprocal(rinv[:, :], ov[:, :, HD]).then_inc(s["rinv_s"], 1)
                need(dve, "rinv_s", B + 1)
                need(dve, "a_T", B)
                v.tensor_tensor(an[:, 0:C].rearrange("p (h d) -> p h d", d=HD), ov[:, :, 0:HD],
                                rinv[:, :].unsqueeze(2).to_broadcast([P, HEADS, HD]),
                                ALU.mult).then_inc(s["an_s"], 1)
                need(dve, "an_s", B + 1)

            def attention_residual(a, t, B, j):
                need(dve, "proj_mm", B + 1)
                if j == 0:
                    need(dve, "g_att_ld", 16 * (a + 1))
                v.tensor_tensor(tmp[:, :], SMALL[:, 0:C], g_att[:, j, :], ALU.mult).then_inc(s["att_t"], 1)
                need(dve, "att_t", B + 1)
                v.tensor_tensor(xt(t), xt(t), tmp[:, :], ALU.add).then_inc(s["x_att"], 1)

            def gating(g):
                n = 4 * g
                need(dve, "lg_T", g + 1)
                need(dve, "cw_b", g)
                v.tensor_copy(lg[:, :, :].rearrange("p j e -> p (j e)"),
                              SMALL[:, 0:G * EXPERTS]).then_inc(s["gate_s"], 1)
                need(dve, "gate_s", n + 1)
                v.tensor_reduce(lmax[:, :], lg[:, :, :], AX.X, ALU.max)
                for e in range(EXPERTS):
                    for lo, hi, op in ((0, e, ALU.is_gt), (e + 1, EXPERTS, ALU.is_ge)):
                        if lo < hi:
                            last = v.tensor_tensor(beat[:, e, :, lo:hi],
                                                   lg[:, :, e:e + 1].to_broadcast([P, G, hi - lo]),
                                                   lg[:, :, lo:hi], op)
                last.then_inc(s["gate_s"], 1)
                need(dve, "gate_s", n + 2)
                v.tensor_tensor(dl[:, :, :], lg[:, :, :],
                                lmax[:, :].unsqueeze(2).to_broadcast([P, G, EXPERTS]),
                                ALU.subtract).then_inc(s["gate_e"], 1)
                v.tensor_reduce(cnt[:, :, :], beat[:, :, :, :].rearrange("p b j e -> p j e b"),
                                AX.X, ALU.add).then_inc(s["gate_s"], 1)
                need(dve, "gate_s", n + 3)
                v.tensor_scalar(sel[:, :, :], cnt[:, :, :], 1.5, None, ALU.is_lt).then_inc(s["gate_s"], 1)
                need(dve, "gate_s", n + 4)

            def mixing(g):
                need(dve, "gate_x", g + 1)
                v.tensor_tensor(es[:, :, :], ex[:, :, :], sel[:, :, :], ALU.mult).then_inc(s["cw_b"], 1)
                need(dve, "cw_b", g + 1)
                v.tensor_reduce(den[:, :], es[:, :, :], AX.X, ALU.add).then_inc(s["mix_s"], 1)
                need(dve, "mix_s", 2 * g + 1)
                v.reciprocal(rden[:, :], den[:, :]).then_inc(s["mix_s"], 1)
                need(dve, "mix_s", 2 * g + 2)
                need(dve, "b2_s", 12 * g)
                v.tensor_tensor(cw[:, :, :], es[:, :, :],
                                rden[:, :].unsqueeze(2).to_broadcast([P, G, EXPERTS]),
                                ALU.mult).then_inc(s["cw_s"], 1)

            def experts_residual(g, j):
                t = G * g + j
                if j == 0:
                    need(dve, "cw_s", g + 1)
                    need(dve, "g_mlp_ld", 16 * (g + 1))
                need(dve, "b2_s", 3 * t + 3)
                for e in range(EXPERTS):
                    if e % 2 == 0:
                        need(dve, "w2_mm", 2 * t + e // 2 + 1)
                    need(dve, "acc_s", 4 * t + e)
                    src = bank[O_BANK[e // 2]][:, (e % 2) * C:(e % 2 + 1) * C]
                    v.scalar_tensor_tensor(acc[:, :], src, cw[:, j, e:e + 1],
                                           bias2[:, j % 2, :] if e == 0 else acc[:, :],
                                           ALU.mult, ALU.add).then_inc(s["acc_s"], 1)
                need(dve, "acc_s", 4 * t + 4)
                v.tensor_tensor(tmp[:, :], acc[:, :], g_mlp[:, j, :], ALU.mult).then_inc(s["acc_g"], 1)
                need(dve, "acc_g", t + 1)
                v.tensor_tensor(xt(t), xt(t), tmp[:, :], ALU.add).then_inc(s["x_mlp"], 1)

            def mlp_residual(g, j):
                t = G * g + j
                if j == 0:
                    need(dve, "g_mlp_ld", 16 * (NG + g + 1))
                need(dve, "x_mlp", BATCH + t)
                need(dve, "f2_mm", t + 1)
                v.tensor_tensor(tmp[:, :], bank[O_BANK[j % 2]][:, 0:C], g_mlp[:, j, :],
                                ALU.mult).then_inc(s["f2_t"], 1)
                need(dve, "f2_t", t + 1)
                v.tensor_tensor(xt(t), xt(t), tmp[:, :], ALU.add).then_inc(s["x_mlp"], 1)

            def setup():
                v.memset(sqr[0][:, :], 0.0)
                v.memset(sqr[1][:, :], 0.0).then_inc(s["zeroed"], 1)
                v.memset(c_nat[:, C:C + 1], 1.0)
                step(v.memset(mask[:, :], 0.0))
                for k in range(NS):
                    v.memset(mask[SLOT * k:SLOT * k + CR, 0:1], 1.0)
                    v.memset(mask[SLOT * k:SLOT * k + CR + 1, 1:2], 1.0)
                v.memset(KA[64:96, :, :, :], -1.0)
                v.memset(hid4[64:65, :], 1.0)
                v.memset(w2_sb[:, MT1 - 1:MT1 + 1, :], 0.0)
                v.memset(w2_sb[:, 3 * MT1 - 1:3 * MT1 + 1, :], 0.0)
                v.memset(s1r, 0.0)
                v.memset(sfr, 0.0).then_inc(s["zeroed"], 1)
                dve.wait_ge(s["silu"], 1)
                step(v.tensor_scalar(c_tmp[:, 0:C], c_tmp[:, C:2 * C], 1.0, None, ALU.add))
                step(v.reciprocal(c_tmp[:, 2 * C:3 * C], c_tmp[:, 0:C]))
                v.tensor_tensor(c_nat[:, 0:C], c_nat[:, 0:C], c_tmp[:, 2 * C:3 * C],
                                ALU.mult).then_inc(s["silu"], 1)
                norm(0, 0)
                modulation(0)
                weights(0)
                h_rest(0, 0)

            def attention(what, i, L, g, start=False):
                a = NG * L + g
                B = G * a
                if what == "NORM":
                    norm(*after(2 * L, g))
                if what == "H_REST":
                    h_rest(*after(2 * L, g))
                if what == "QK":
                    part_r(a if start else a + 1, i)
                if what == "MAX":
                    row_max(B + i // QUADS, i % QUADS)
                    if i % QUADS == QUADS - 1:
                        max_split(B + i // QUADS)
                    if start and i == LEAD - 1 and L == 0:
                        modulation(1)
                        weights(1)
                if what == "OUT_T":
                    normalise(B + i)
                if what == "PROJ":
                    attention_residual(a + i // G, G * g + i, B + i, i % G)

            def mlp(what, i, L, g):
                if what == "NORM":
                    norm(*after(2 * L + 1, g))
                if what == "H_REST":
                    h_rest(*after(2 * L + 1, g))
                if what == "LOGITS_T":
                    gating(g)
                if what == "MIX":
                    mixing(g)
                if what == "DOWN":
                    (experts_residual if L == 0 else mlp_residual)(g, i)

            phases(dve, setup, attention, mlp)

        @block.tensor
        def _(pe):
            te = nc.tensor

            def transposes(ph, g, rest):
                n = NG * ph + g
                if rest:
                    need(pe, "h_main", n + 1)
                else:
                    need(pe, "normed", n + 1)
                    need(pe, "h_rest", n)
                for j in range(G):
                    src = xr[:, j, :, :].rearrange("p s c -> p (s c)") if rest else xn[:, j, :]
                    last = te.transpose(PREP[:, j * SEQ:(j + 1) * SEQ], src, ident[:, :])
                last.then_inc(s["T_done"], 1)

            def product(dst, hi, lo, rest, cols):
                te.matmul(dst, lo[:, cols], hhi[:, :], start=True, stop=False)
                te.matmul(dst, hi[:, cols], hlo[:, :], start=False, stop=False)
                te.matmul(dst, rest[:, cols], hR[:, :], start=False, stop=False)
                return te.matmul(dst, hi[:, cols], hhi[:, :], start=False, stop=True)

            def qk(ph, g, a, L, t):
                if t == 0:
                    need(pe, "h_ready", NG * ph + g + 1)
                    need(pe, "qk_weights", L + 1)
                need(pe, "part_r", 3 * a + t)
                cols = slice(t * ROWS8, (t + 1) * ROWS8 if t < 2 else 2 * C)
                product(PREP[0:rows(t), :], wqk_hi[L], wqk_lo[L], wqk_r[L], cols).then_inc(s["qk_mm"], 1)

            def values(a, L, k):
                if k == 0:
                    need(pe, "part_r", 3 * a + 3)
                else:
                    need(pe, "v_ready", 2 * a + 1)
                for c, j in enumerate(((0, 1, 2), (3,))[k]):
                    dst, tok = PREP[:, c * C:(c + 1) * C], slice(j * SEQ, (j + 1) * SEQ)
                    te.matmul(dst, h32[:, tok], sq[L][:, 2 * C:3 * C], start=True, stop=False)
                    last = te.matmul(dst, hR[:, tok], wv_r[L][:, :], start=False, stop=True)
                last.then_inc(s["v_mm"], 1)

            def scores(a, B, j, q):
                qi = 4 * B + q
                need(pe, "max_s", qi - 1)
                if q == 0:
                    pe.wait_ge(qk_ld[j], 96 * (a + 1))
                for i in range(HQ):
                    h = HQ * q + i
                    last = te.matmul(bank[S_BANK[q % 2]][:, i * SEQ:(i + 1) * SEQ],
                                     QA[0:SROWS, j, h, :], KA[0:SROWS, j, h, :], start=True, stop=True)
                last.then_inc(s["s_mm"], 1)

            def scores_T(B, j, q):
                need(pe, "exp_s", 4 * B + q - 1)
                if q == 0:
                    need(pe, "m_ld", 16 * (B + 1))
                for i in range(HQ):
                    h = HQ * q + i
                    last = te.matmul(bank[ST_BANK[q % 2]][:, i * SEQ:(i + 1) * SEQ],
                                     KA[0:MROWS, j, h, :], QA[0:MROWS, j, h, :], start=True, stop=True)
                last.then_inc(s["st_mm"], 1)

            def weigh(a, B, j, q):
                need(pe, "exp_s", 4 * B + q + 1)
                if q == 0:
                    need(pe, "o_ev", B - 1)
                    need(pe, "v_ready", 2 * a + (2 if j == 3 else 1))
                for i in range(HQ):
                    last = te.matmul(bank[O_BANK[j % 2]][SLOT * i:SLOT * (i + 1), q * SEQ:(q + 1) * SEQ],
                                     V[:, j, HQ * q + i, :], pr[:, q % 2, i * SEQ:(i + 1) * SEQ],
                                     start=True, stop=True)
                last.then_inc(s["pv_mm"], 1)

            def out_T(B):
                need(pe, "o_ev", B + 1)
                need(pe, "att_t", B)
                for q in range(QUADS):
                    last = te.transpose(SMALL[:, q * SEQ:(q + 1) * SEQ], osb[:, q * SEQ:(q + 1) * SEQ],
                                        ident[:, :])
                last.then_inc(s["o_T"], 1)

            def max_T(B, start):
                need(pe, "msplit", 2 * B + 2)
                need(pe, "an_s", B - 1)
                need(pe, "mt_c", B)
                te.transpose(SMALL[0:2 * HEADS, 0:SEQ // 2].bitcast(BF16),
                             mp[:, :, :].rearrange("p s h -> p (s h)"), identb[:, :]).then_inc(s["mt_mm"], 1)

            def att_T(B, j, last_one):
                need(pe, "an_s", B + 1)
                if not last_one:
                    need(pe, "mt_c", B + 3)
                te.transpose(SMALL[:, 0:SEQ], an[:, 0:CM], ident[:, :])
                te.transpose(SMALL[0:CR + 1, SEQ:2 * SEQ], an[:, CM:C + 1], ident[:, :]).then_inc(s["a_T"], 1)

            def project(L, B):
                need(pe, "a_c", B + 1)
                te.matmul(SMALL[:, 0:C], aTr[:, :], wo_r[L][:, :], start=True, stop=False)
                te.matmul(SMALL[:, 0:C], aT[:, :], wo_m[L][:, :], start=False,
                          stop=True).then_inc(s["proj_mm"], 1)

            def modulation(L):
                pe.wait_ge(s[f"ld_ada{L}"], NADA)
                bk = bank[MOD_BANK[L]]

                def modulate(dst, lo, n):
                    te.matmul(dst, ada_m[L][:, lo:lo + n], cT[:, :], start=True, stop=False)
                    return te.matmul(dst, ada_r[L][:, lo:lo + n], cTr[:, :], start=False, stop=True)

                for i, k in enumerate(MSET):
                    modulate(bk[:, 16 * i:16 * i + 16], k * C, CM)
                    for n in range(NS):
                        last = modulate(bk[SLOT * n:SLOT * (n + 1), 64 + 16 * i:80 + 16 * i],
                                        k * C + CM, SLOT)
                last.then_inc(s["mod_mm"], 1)
                for w, k in enumerate((2, 5)):
                    dst = bank[O_BANK[L]][0:BATCH, w * C:(w + 1) * C]
                    te.matmul(dst, cT[:, :], ada_m[L][:, k * C:(k + 1) * C], start=True, stop=False)
                    te.matmul(dst, cTr[:, :], ada_r[L][:, k * C:(k + 1) * C], start=False,
                              stop=True).then_inc(s["mod_mm"], 1)

            def setup():
                pe.wait_ge(s["pooled"], 4)
                pe.wait_ge(s["silu"], 2)
                te.transpose(SMALL[:, 0:BATCH], c_nat[:, 0:CM], ident[0:BATCH, 0:BATCH])
                te.transpose(SMALL[0:CR + 1, BATCH:2 * BATCH], c_nat[:, CM:C + 1],
                             ident[0:BATCH, 0:BATCH]).then_inc(s["cond_T"], 1)
                pe.wait_ge(s["cond_c"], 1)
                modulation(0)
                transposes(0, 0, False)
                transposes(0, 0, True)

            def attention(what, i, L, g, start=False):
                a = NG * L + g
                B = G * a
                if start and what == "QK" and i == 0 and L == 1:
                    need(pe, "gelu", MT0 * NG)
                    need(pe, "acc_s", 4 * BATCH)
                    need(pe, "gate_s", 4 * NG)
                if L == 0 and isinstance(g, int) and g == 0 and not start:
                    if what == "SCORE" and i == 1:
                        need(pe, "mod_read", 2)
                    if what == "PV" and i == 0:
                        need(pe, "gate_c", 4)
                    if what == "PROJ" and i == 0:
                        need(pe, "ld_wo", 16 * 6)
                    if what == "OUT_T" and i == 0:
                        need(pe, "mt_c", 2)
                if what == "H_MAIN":
                    need(pe, "v_ready", 2 * a + 2)
                    transposes(*after(2 * L, g), False)
                if what == "H_REST":
                    transposes(*after(2 * L, g), True)
                if what == "QK":
                    if start:
                        qk(2 * L, g, a, L, i)
                    else:
                        qk(2 * L, g + 1, a + 1, L, i)
                if what == "V":
                    values(a if start else a + i[0], L, i[1])
                    if start and L == 0:
                        modulation(1)
                if what == "MAX":
                    scores(a + i // (QUADS * G), B + i // QUADS, i // QUADS % G, i % QUADS)
                if what == "SCORE":
                    scores_T(B + i // QUADS, i // QUADS, i % QUADS)
                if what == "PV":
                    weigh(a + i // (QUADS * G), B + i // QUADS, i // QUADS % G, i % QUADS)
                if what == "OUT_T":
                    out_T(B + i)
                if what == "MAX_T":
                    max_T(B + i, start)
                if what == "ATT_T":
                    att_T(B + i, i % G, isinstance(g, int) and g == NG - 1 and i >= G - 2)
                if what == "PROJ":
                    project(L, B + i)

            def up(L, g, m):
                count, done, tiles = ("w1_mm", "gelu", MT0) if L == 0 else ("f1_mm", "f1_gelu", MT1)
                if m == 0:
                    need(pe, "h_ready", NG * (2 * L + 1) + g + 1)
                    need(pe, "split_s", 9)
                    need(pe, "exp_s", 64 * (L + 1))
                    need(pe, "max_s", 64 * (L + 1))
                need(pe, done, tiles * g + (m - 3 if m >= 4 else 0))
                n = P if L == 0 or m < 4 else HID - 4 * P
                hi, lo, rest = (w1_hi, w1_lo, w1_r) if L == 0 else (f1_hi, f1_lo, f1_r)
                last = product(bank[m % 4][0:n, :], hi, lo, rest, slice(m * P, m * P + n))
                last.then_inc(s[count], 1)

            def down_experts(g, j):
                t = G * g + j
                tok = slice(j * SEQ, (j + 1) * SEQ)
                for pair in range(2):
                    if j == 0:
                        need(pe, "gelu", MT0 * g + MT0 // 2 * (pair + 1))
                    need(pe, "acc_s", 4 * t - 2 + 2 * pair)
                    for e in (2 * pair, 2 * pair + 1):
                        dst = bank[O_BANK[pair]][:, (e % 2) * C:(e % 2 + 1) * C]
                        for i in range(MT1):
                            at = (e * HID // P + i) * GT + j * SEQ
                            last = te.matmul(dst, hid[:, at:at + SEQ], w2_sb[:, MT1 * e + i, :],
                                             start=(i == 0), stop=(i == MT1 - 1))
                    last.then_inc(s["w2_mm"], 1)

            def down(g, j):
                t = G * g + j
                if j == 0:
                    need(pe, "f1_gelu", MT1 * (g + 1))
                need(pe, "f2_t", t - 1)
                dst = bank[O_BANK[j % 2]][:, 0:C]
                for m in range(MT1):
                    n = P if m < 4 else HID - 4 * P + 1
                    src = hid[:, m * GT + j * SEQ:m * GT + (j + 1) * SEQ] if m < 4 \
                        else hid4[0:n, j * SEQ:(j + 1) * SEQ]
                    last = te.matmul(dst, src, f2_sb[0:n, m, :], start=(m == 0), stop=(m == MT1 - 1))
                last.then_inc(s["f2_mm"], 1)

            def mlp(what, i, L, g):
                ph = 2 * L + 1
                if what == "LOGITS":
                    need(pe, "h_ready", NG * ph + g + 1)
                    need(pe, "split_s", 9)
                    need(pe, "att_t", BATCH)
                    need(pe, "gate_s", 4 * g)
                    product(SMALL[0:EXPERTS, :], wg_hi, wg_lo, wg_r,
                            slice(0, EXPERTS)).then_inc(s["gl_mm"], 1)
                if what == "LOGITS_T":
                    for j in range(G):
                        last = te.transpose(SMALL[:, j * EXPERTS:(j + 1) * EXPERTS],
                                            lgT[:, j * SEQ:(j + 1) * SEQ], ident[0:EXPERTS, 0:EXPERTS])
                    last.then_inc(s["lg_T"], 1)
                if what == "UP":
                    if L == 0 and i == 3:
                        need(pe, "gl_c", g + 1)
                    up(L, g, i)
                if what == "DOWN":
                    if isinstance(g, int) and g == 0 and i == 0:
                        pe.wait_ge(s["ld_w2"], NW2)
                        need(pe, "o_ev", BATCH * (L + 1))
                    (down_experts if L == 0 else down)(g, i)
                if what == "H_MAIN":
                    transposes(*after(ph, g), False)
                if what == "H_REST":
                    transposes(*after(ph, g), True)

            phases(pe, setup, attention, mlp)


_INS = ["x", "cond_1152",
        "L0_cond_w_adaln", "L0_cond_b_adaln", "L0_cond_w_qkv", "L0_cond_b_qkv", "L0_cond_w_proj",
        "L0_cond_b_proj", "L0_cond_w_gate", "L0_cond_w1", "L0_cond_b1", "L0_cond_w2", "L0_cond_b2",
        "L1_cond_ln1_w", "L1_cond_ln1_b", "L1_cond_wq", "L1_cond_wk", "L1_cond_wv", "L1_cond_wo",
        "L1_cond_wo_b", "L1_cond_ln2_w", "L1_cond_ln2_b", "L1_cond_fc1_w", "L1_cond_fc1_b",
        "L1_cond_fc2_w", "L1_cond_fc2_b", "L1_cond_ada_w", "L1_cond_ada_b"]


def kernel(**inputs):
    import numpy as np
    import concourse.bacc as bacc
    from concourse.bass_utils import run_bass_kernel_spmd

    nc = bacc.Bacc("TRN2", target_bir_lowering=False, num_devices=1)
    arrays, args = {}, []
    for name in _INS:
        a = np.ascontiguousarray(inputs[name])
        arrays[f"in_{name}"] = a
        args.append(nc.dram_tensor(f"in_{name}", a.shape, mybir.dt.from_np(a.dtype),
                                   kind="ExternalInput").ap())
    out = nc.dram_tensor("out", (BATCH, SEQ, C), F32, kind="ExternalOutput").ap()
    build(nc, *args, out)
    return run_bass_kernel_spmd(nc, [arrays], core_ids=[0]).results[0]["out"]
```

```python
from contextlib import ExitStack

import concourse.bass as bass
from concourse import mybir

ALU = mybir.AluOpType
ACT = mybir.ActivationFunctionType
AX = mybir.AxisListType
F32 = mybir.dt.float32
F32R = mybir.dt.float32r
BF16 = mybir.dt.bfloat16

P = 128
BATCH, SEQ, C = 16, 128, 144
HEADS, HD = 16, 9
EXPERTS, HID = 4, 576
SCALE = HD ** -0.5
EPS = (1e-6, 1e-5)

CM = P
CR = C - CM
SLOT = 32
NS = P // SLOT
G = 4
NG = BATCH // G
GT = G * SEQ
QUADS = 4
HQ = HEADS // QUADS
AHEAD = 5
LEAD = 6
PARTS = 3
SROWS = PARTS * PARTS * HD
MROWS = SROWS + 2
CT = HD * HEADS
ROWS8 = 8 * HEADS
VW = 32
MT0 = EXPERTS * HID // P
MT1 = 5
MSET = (0, 1, 3, 4)


def build(nc, x, cond, w_adaln, b_adaln, w_qkv, b_qkv, w_proj, b_proj, w_gate, w1, b1, w2, b2,
          ln1_w, ln1_b, wq, wk, wv, wo, wo_b, ln2_w, ln2_b, fc1_w, fc1_b, fc2_w, fc2_b,
          ada_w, ada_b, out):
    qk_dram = nc.dram_tensor("qk_scratch", [G, 2, PARTS, CT, SEQ], BF16).ap()
    gate_dram = nc.dram_tensor("gate_scratch", [2, 2, BATCH, C], F32).ap()

    with ExitStack() as ctx:
        def sb(name, shape, dt=F32):
            return ctx.enter_context(nc.sbuf_tensor(name, shape, dt))

        def sem(name):
            return ctx.enter_context(nc.semaphore(name))

        bank = [ctx.enter_context(nc.psum_tensor(f"bank{i}", [P, 512], F32)) for i in range(8)]
        S_BANK, ST_BANK, O_BANK, PREP, SMALL = (0, 1), (2, 3), (4, 5), bank[6], bank[7]
        MOD_BANK = (bank[0][:, 0:P], PREP[:, 0:P])
        GATE_BANK = (bank[4][:, 0:2 * C], PREP[:, P:P + 2 * C])
        START_BANK = (PREP, bank[1], bank[2])

        xs = sb("xs", [P, BATCH * C])
        ident = sb("ident", [P, P])
        identb = sb("identb", [P, P], BF16)

        stats = sb("stats", [P, G, 6])
        msum, mdif, sq2, mean, vdif, vown = [sb(n, [P, G]) for n in
                                             "msum mdif sq2 mean vdif vown".split()]
        rstd = sb("rstd", [P, G])
        var_eps = sb("var_eps", [P, G])
        minus_half = sb("minus_half", [P, G])
        xn = sb("xn", [P, G, CM])
        xr = sb("xr", [P, G, NS, SLOT])
        h32 = sb("h32", [P, GT])
        hhi = sb("hhi", [P, GT], F32R)
        hlo = sb("hlo", [P, GT], F32R)
        r32 = sb("r32", [P, GT])
        hR = sb("hR", [P, GT], F32R)

        a_main = sb("a_main", [P, 4, BATCH])
        b_main = sb("b_main", [P, 4, BATCH])
        a_rest = sb("a_rest", [P, 4, BATCH])
        b_rest = sb("b_rest", [P, 4, BATCH])
        mask = sb("mask", [P, 2])
        lnm = sb("lnm", [P, 4])
        lnr = sb("lnr", [P, 4])
        c_nat = sb("c_nat", [BATCH, C + 1])
        c_tmp = sb("c_tmp", [BATCH, 3 * C])
        cT = sb("cT", [P, BATCH])
        cTr = sb("cTr", [CR + 1, BATCH])
        gates = sb("gates", [BATCH, 2, 2 * C])
        g_att = sb("g_att", [P, G, C])
        g_mlp = sb("g_mlp", [P, G, C])

        sq = [sb(f"sq{l}", [P, 3 * C]) for l in range(2)]
        sqr = [sb(f"sqr{l}", [P, 3 * C]) for l in range(2)]
        bw = sb("bw", [P, EXPERTS, C])
        bw_flat = bw[:, :, :].rearrange("p e c -> p (e c)")
        wp32, wr32 = bw_flat[:, 0:2 * C], bw_flat[:, 2 * C:]
        wqk_hi = [sb(f"wqk_hi{l}", [P, 2 * C], F32R) for l in range(2)]
        wqk_lo = [sb(f"wqk_lo{l}", [P, 2 * C], F32R) for l in range(2)]
        wqk_r = [sb(f"wqk_r{l}", [P, 2 * C], F32R) for l in range(2)]
        wv_r = [sb(f"wv_r{l}", [P, C], F32R) for l in range(2)]
        wo_m = [sb(f"wo_m{l}", [P, C]) for l in range(2)]
        wo_r = [sb(f"wo_r{l}", [CR + 1, C]) for l in range(2)]

        N0, N1 = EXPERTS * HID, HID
        w1_hi = sb("w1_hi", [P, N0], F32R)
        w1_lo = sb("w1_lo", [P, N0], F32R)
        w1_r = sb("w1_r", [P, N0], F32R)
        f1_hi = sb("f1_hi", [P, N1], F32R)
        f1_lo = sb("f1_lo", [P, N1], F32R)
        f1_r = sb("f1_r", [P, N1], F32R)
        sg = sb("sg", [P, EXPERTS])
        sgr = sb("sgr", [P, EXPERTS])
        wg_hi = sb("wg_hi", [P, EXPERTS], F32R)
        wg_lo = sb("wg_lo", [P, EXPERTS], F32R)
        wg_r = sb("wg_r", [P, EXPERTS], F32R)
        w2_sb = sb("w2_sb", [P, EXPERTS * MT1, C])
        f2_sb = sb("f2_sb", [P, MT1, C])
        b2_sb = sb("b2_sb", [P, EXPERTS, C])

        hid = sb("hid", [P, MT0 * GT])
        hid4 = sb("hid4", [P, GT])
        NA = 6 * C
        ada_m = [hid[:, (2 * l) * NA:(2 * l + 1) * NA] for l in range(2)]
        ada_r = [hid[0:CR + 1, (2 * l + 1) * NA:(2 * l + 2) * NA] for l in range(2)]
        o = 4 * NA
        s1 = hid[:, o:o + N0]
        s1r = hid[:, o + N0:o + 2 * N0]
        o += 2 * N0
        sf = hid[:, o:o + N1]
        sfr = hid[:, o + N1:o + 2 * N1]

        parts = sb("parts", [P, 3, PARTS, GT], BF16)
        resid = sb("resid", [P, GT])
        QA = sb("QA", [P, G, HEADS, SEQ], BF16)
        KA = sb("KA", [P, G, HEADS, SEQ], BF16)
        V = sb("V", [P, G, HEADS, VW])
        v_last = sb("v_last", [P, C])
        mx = sb("mx", [P, HEADS])
        mp = sb("mp", [P, 2, HEADS], BF16)
        mT = sb("mT", [2 * HEADS, SEQ], BF16)
        pr = sb("pr", [P, 2, 512])
        osb = sb("osb", [P, 512])
        rinv = sb("rinv", [P, HEADS])
        an = sb("an", [P, C + 1])
        aT = sb("aT", [P, SEQ])
        aTr = sb("aTr", [CR + 1, SEQ])
        tmp = sb("tmp", [P, C])

        lgT = sb("lgT", [EXPERTS, GT])
        lg = sb("lg", [P, G, EXPERTS])
        lmax = sb("lmax", [P, G])
        beat = sb("beat", [P, EXPERTS, G, EXPERTS])
        cnt = sb("cnt", [P, G, EXPERTS])
        sel = sb("sel", [P, G, EXPERTS])
        dl = sb("dl", [P, G, EXPERTS])
        ex = sb("ex", [P, G, EXPERTS])
        es = sb("es", [P, G, EXPERTS])
        den = sb("den", [P, G])
        rden = sb("rden", [P, G])
        cw = sb("cw", [P, G, EXPERTS])
        bw2 = sb("bw2", [P, 2, C])
        bias2 = sb("bias2", [P, 2, C])
        acc = sb("acc", [P, C])

        names = """ld_x0 ld_x ld_c ld_ada0 ld_ada1 ld_ln ld_qkv0 ld_qkv1 ld_wo ld_w1 ld_f1 ld_w2
            zeroed pooled silu cond_T cond_c mod_mm mod_done gate_c gate_st wsplit qk_weights split_s
            stats_s sums_s vars_s aggr_s rstd_s normed T_done h_main h_hi h_rest r_hi h_ready
            qk_mm part_a part_r part_b part_c scr_w v_mm v_ready v3_ready
            s_mm max_s msplit mt_mm mt_c m_ld st_mm exp_s pv_mm o_ev o_T rinv_s an_s a_T a_c
            proj_mm att_t x_att g_att_ld0 g_att_ld1 g_mlp_ld gate_x cw_b mix_s mod_read
            gl_mm gl_c lg_T gate_s gate_e cw_s b2_s w1_mm gelu w2_mm acc_s acc_g x_mlp
            f1_mm f1_gelu f2_mm f2_t st_out""".split()
        s = {n: sem(n) for n in names}
        qk_ld = [sem(f"qk_ld{j}") for j in range(G)]

        def need(eng, name, value):
            if isinstance(value, int) and value <= 0:
                return
            eng.wait_ge(s[name], value)

        def xt(t):
            return xs[:, bass.ds(t * C, C)] if not isinstance(t, int) else xs[:, t * C:(t + 1) * C]

        def col(tile, ph, t):
            return tile[:, ph, t:t + 1] if isinstance(t, int) else tile[:, ph, bass.ds(t, 1)]

        def attention_order(first, last, mod_too=False):
            tail = mlp_prefix(last)
            for pos in range(0 if first else -AHEAD, QUADS * (G + 1) if last else QUADS * G - AHEAD):
                k, q = pos // QUADS, pos % QUADS
                own = k < G
                if pos + LEAD < QUADS * G or (own and not last):
                    yield "MAX", pos + LEAD
                if own:
                    yield "SCORE", pos
                if not last and pos in (1, 2, 3):
                    yield "QK_PARTS", pos - 1
                if not last and pos in (4, 8):
                    yield "LOAD", (1, pos // 4 - 1)
                if pos == -4:
                    yield "LOAD", (0, 2)
                if pos - 1 < QUADS * G and not (first and pos == 0):
                    yield "PV", pos - 1
                if q == 2 and (k + 1 < G or (own and not last)):
                    yield "MAX_T", k + 1
                if not (first and k < 1) and q > 0:
                    yield ("OUT_T", "ATT_T", "PROJ")[q - 1], k - 1
                if q == 2 and (k + 1 < G or (own and not last)):
                    yield "MAX_STORE", k + 1
                if pos == -5:
                    yield "NORM", 1
                if pos == -4:
                    yield "V", (0, 0)
                    yield "V", (0, 1)
                    yield "NORM_APPLY", 1
                if pos == -3:
                    yield "H_MAIN", 1
                if pos == -2:
                    yield "H_REST", 1
                if pos == -1:
                    yield "LOAD", (0, 3)
                    yield "GATE_LOAD", 0
                    yield "H_SPLIT", 1
                if pos == 0:
                    yield "V3", 0
                if pos == 4:
                    yield "GATE_LOAD", 1
                if not last and pos in (0, 1, 2):
                    yield "QK", pos
                if mod_too and 5 <= pos < 5 + MOD_STEPS:
                    yield "MOD", pos - 5
                if not own:
                    yield from tail[q]

        MOD_STEPS = 5

        def mlp_prefix(last):
            if not last:
                return None
            return [[("MLP", s_) for s_ in part] for part in
                    (OVERLAP[0:2], OVERLAP[2:3], OVERLAP[3:4], OVERLAP[4:])]

        OVERLAP = [("GATE_LOAD", 0), ("UP", 0), ("UP", 1), ("UP", 2), ("UP", 3), ("NORM", 1), ("NORM_APPLY", 1)]

        def attention_start(L):
            if L == 0:
                for t in range(3):
                    yield "QK", t
                    yield "QK_PARTS", t
                for j in range(G):
                    yield "LOAD", (0, j)
                yield "V", (0, 0)
                yield "V", (0, 1)
            yield "NORM", 1
            yield "NORM_APPLY", 1
            for p in range(LEAD):
                yield "MAX", p
                if p == 2:
                    yield "H_MAIN", 1
                if p == 4:
                    yield "H_REST", 1
                if p == 3:
                    yield "MAX_T", 0
                    yield "MAX_STORE", 0
            yield "H_SPLIT", 1
            yield "GATE_LOAD", 0

        def mlp_order(L, first, last):
            if not first:
                yield "GATE_LOAD", 0
                if not (last and L == 1):
                    yield "NORM", 1
                    yield "NORM_APPLY", 1
            tiles = MT0 if L == 0 else MT1
            for m in range(tiles):
                if L == 0 and m == 4:
                    yield "LOGITS", 0
                if not (first and m < 4):
                    yield "UP", m
                if L == 0 and m == 6:
                    yield "LOGITS_T", 0
                if L == 0 and m == 10:
                    yield "MIX", 0
            if L == 1:
                between = {0: [("H_MAIN", 1)], 1: [("H_REST", 1)], 2: [("H_SPLIT", 1)]}
            else:
                between = {1: [("H_MAIN", 1)], 2: [("H_REST", 1)], 3: [("H_SPLIT", 1)]}
            if last:
                between = {-1: [("H_MAIN", 1)], 0: [("H_REST", 1)], 1: [("H_SPLIT", 1)],
                           2: [("START", ("QK", 0))],
                           3: [("START", ("QK_PARTS", 0)), ("START", ("QK", 1))],
                           4: [("START", ("QK_PARTS", 1)), ("START", ("QK", 2))],
                           5: [("START", ("QK_PARTS", 2)), ("START", ("V", (0, 0)))]
                           + [("START", ("LOAD", (0, j))) for j in range(G)],
                           6: [("START", ("V", (0, 1)))]} if L == 0 else {}
            yield from between.get(-1, ())
            for i in range(G * (2 - L)):
                yield "DOWN", i
                yield from between.get(i, ())

        def phases(eng, setup, attention, mlp):
            def group(order, stage, L, g):
                for what, i in order:
                    if what == "MLP":
                        mlp(*i, L, 0)
                    elif what == "START":
                        attention(*i, L + 1, 0, True)
                    else:
                        stage(what, i, L, g)

            setup()
            for L in range(2):
                for what, i in attention_start(L):
                    attention(what, i, L, 0, True)
                group(attention_order(True, False, mod_too=L == 0), attention, L, 0)
                with eng.Fori(1, NG - 1) as g:
                    group(attention_order(False, False), attention, L, g)
                group(attention_order(False, True), attention, L, NG - 1)
                group(mlp_order(L, True, False), mlp, L, 0)
                with eng.Fori(1, NG - 1) as g:
                    group(mlp_order(L, False, False), mlp, L, g)
                group(mlp_order(L, False, True), mlp, L, NG - 1)

        def after(ph, g):
            return (ph + 1, 0) if isinstance(g, int) and g == NG - 1 else (ph, g + 1)

        def inputs_used(eng, ph, g):
            if isinstance(g, int) and g == 0:
                ph, g = ph - 1, NG
            if ph in (0, 2):
                need(eng, "v_mm", 2 * (NG * (ph // 2) + g))
            elif ph > 0:
                need(eng, *(("w1_mm", MT0 * g) if ph == 1 else ("f1_mm", MT1 * g)))

        def rows(t):
            return P if t > 0 else 2 * HEADS

        NADA = 16 * 3
        QK_LOADS = 16 * (1 + PARTS)
        NW2 = 16 * (2 * EXPERTS + 4)
        NLN = 16 * (4 + 4 * NS)
        NQKV = (16 * (1 + 2 * NS), 16 * (3 + 3 * NS))
        block = ctx.enter_context(nc.Block())

        @block.sync
        def _(sp):
            xv = x.rearrange("b p c -> p b c")
            xd = xs[:, :].rearrange("p (b c) -> p b c", c=C)
            sp.dma_start(c_nat[:, 0:C], cond).then_inc(s["ld_c"], 16)
            sp.dma_start(xd[:, 0:G], xv[:, 0:G]).then_inc(s["ld_x0"], 16)

            def load_ada(L, w, b):
                done = s[f"ld_ada{L}"]
                sp.dma_start(ada_m[L], w[0:CM, :]).then_inc(done, 16)
                sp.dma_start(ada_r[L][0:CR, :], w[CM:C, :]).then_inc(done, 16)
                sp.dma_start(ada_r[L][CR:CR + 1, :], b.unsqueeze(0)).then_inc(done, 16)

            load_ada(0, w_adaln, b_adaln)
            sp.dma_start(sq[0][:, :], w_qkv[0:CM, :]).then_inc(s["ld_qkv0"], 16)
            need(sp, "zeroed", 1)
            for k in range(NS):
                sp.dma_start(sqr[0][SLOT * k:SLOT * k + CR, :], w_qkv[CM:C, :]).then_inc(s["ld_qkv0"], 16)
                sp.dma_start(sqr[0][SLOT * k + CR:SLOT * k + CR + 1, :],
                             b_qkv.unsqueeze(0)).then_inc(s["ld_qkv0"], 16)
            sp.dma_start(xd[:, G:], xv[:, G:]).then_inc(s["ld_x"], 16)

            for L, (w, b) in enumerate(((w_proj, b_proj), (wo, wo_b))):
                sp.dma_start(wo_m[L][:, :], w[0:CM, :]).then_inc(s["ld_wo"], 16)
                sp.dma_start(wo_r[L][0:CR, :], w[CM:C, :]).then_inc(s["ld_wo"], 16)
                sp.dma_start(wo_r[L][CR:CR + 1, :], b.unsqueeze(0)).then_inc(s["ld_wo"], 16)
            load_ada(1, ada_w, ada_b)
            need(sp, "pooled", 1)
            for i, v in enumerate((ln1_w, ln1_b, ln2_w, ln2_b)):
                sp.dma_start(lnm[:, i:i + 1], v[0:CM].unsqueeze(1)).then_inc(s["ld_ln"], 16)
                for k in range(NS):
                    sp.dma_start(lnr[SLOT * k:SLOT * k + CR, i:i + 1],
                                 v[CM:C].unsqueeze(1)).then_inc(s["ld_ln"], 16)

            w1_c = w1.rearrange("e c h -> c e h")

            def load_late(step):
                if step == 0:
                    for i, w in enumerate((wq, wk, wv)):
                        sp.dma_start(sq[1][:, i * C:(i + 1) * C], w[0:CM, :]).then_inc(s["ld_qkv1"], 16)
                        for k in range(NS):
                            sp.dma_start(sqr[1][SLOT * k:SLOT * k + CR, i * C:(i + 1) * C],
                                         w[CM:C, :]).then_inc(s["ld_qkv1"], 16)
                if step == 1:
                    sp.dma_start(s1.rearrange("p (e h) -> p e h", e=EXPERTS), w1_c[0:CM]).then_inc(s["ld_w1"], 16)
                    sp.dma_start(sg[:, :], w_gate[0:CM, :]).then_inc(s["ld_w1"], 16)
                    sp.dma_start(sf, fc1_w[0:CM, :]).then_inc(s["ld_f1"], 16)
                if step == 2:
                    need(sp, "pooled", 5)
                    b1f = b1.rearrange("e h -> (e h)").unsqueeze(0)
                    for k in range(NS):
                        a = SLOT * k
                        sp.dma_start(s1r[a:a + CR, :].rearrange("p (e h) -> p e h", e=EXPERTS),
                                     w1_c[CM:C]).then_inc(s["ld_w1"], 16)
                        sp.dma_start(s1r[a + CR:a + CR + 1, :], b1f).then_inc(s["ld_w1"], 16)
                        sp.dma_start(sgr[a:a + CR, :], w_gate[CM:C, :]).then_inc(s["ld_w1"], 16)
                        sp.dma_start(sfr[a:a + CR, :], fc1_w[CM:C, :]).then_inc(s["ld_f1"], 16)
                        sp.dma_start(sfr[a + CR:a + CR + 1, :], fc1_b.unsqueeze(0)).then_inc(s["ld_f1"], 16)
                if step == 3:
                    half = P // 2
                    for e in range(EXPERTS):
                        m, odd = MT1 * e, e % 2
                        sp.dma_start(w2_sb[:, m + odd:m + odd + 4, :],
                                     w2[e, odd * half:odd * half + 4 * P, :].rearrange("(m p) c -> p m c", p=P)
                                     ).then_inc(s["ld_w2"], 16)
                        if odd:
                            sp.dma_start(w2_sb[half:P, m, :], w2[e, 0:half, :]).then_inc(s["ld_w2"], 16)
                        else:
                            sp.dma_start(w2_sb[0:half, m + 4, :], w2[e, 4 * P:HID, :]).then_inc(s["ld_w2"], 16)
                    sp.dma_start(b2_sb[:, :, :], b2.partition_broadcast(P)).then_inc(s["ld_w2"], 16)
                    sp.dma_start(f2_sb[:, 0:4, :],
                                 fc2_w[0:4 * P, :].rearrange("(m p) c -> p m c", p=P)).then_inc(s["ld_w2"], 16)
                    sp.dma_start(f2_sb[0:HID - 4 * P, 4, :], fc2_w[4 * P:HID, :]).then_inc(s["ld_w2"], 16)
                    sp.dma_start(f2_sb[HID - 4 * P:HID - 4 * P + 1, 4, :],
                                 fc2_b.unsqueeze(0)).then_inc(s["ld_w2"], 16)

            def wait_loads(a):
                if not isinstance(a, int) or a > 0:
                    sp.wait_ge(qk_ld[G - 1], QK_LOADS * a)

            def store_parts(a, t):
                if t == 0:
                    wait_loads(a)
                need(sp, "part_c", 3 * a + t + 1)
                for which, lo, n, row in (((t - 1, 0, ROWS8, 0),) if t > 0 else
                                          ((0, 0, HEADS, ROWS8), (1, HEADS, HEADS, ROWS8))):
                    for p in range(PARTS):
                        sp.dma_start(qk_dram[:, which, p, row:row + n, :].rearrange("j c t -> c j t"),
                                     parts[lo:lo + n, t, p, :].rearrange("c (j t) -> c j t", j=G)
                                     ).then_inc(s["scr_w"], 16)

            def load_qk(a, j):
                slot_free = 16 * a - 16 + 4 * j + 4
                if not isinstance(a, int):
                    slot_free = sp.snap(slot_free)
                need(sp, "st_mm", slot_free)
                if j == 0:
                    need(sp, "scr_w", 192 * (a + 1))
                sp.dma_start(QA[0:SROWS, j, :, :].rearrange("p h t -> p (h t)"),
                             qk_dram[j, 0].rearrange("s (d h) t -> (s d) (h t)", h=HEADS)
                             .partition_broadcast(PARTS)).then_inc(qk_ld[j], 16)
                for p in range(PARTS):
                    r = p * PARTS * HD
                    sp.dma_start(KA[r:r + PARTS * HD, j, :, :].rearrange("p h t -> p (h t)"),
                                 qk_dram[j, 1, p].rearrange("(d h) t -> d (h t)", h=HEADS)
                                 .partition_broadcast(PARTS)).then_inc(qk_ld[j], 16)

            def gate_rows(L, which, g, lo, n):
                t = G * g + lo
                return gate_dram[L, which, t:t + n, :] if isinstance(t, int) \
                    else gate_dram[L, which, bass.ds(t, n), :]

            def load_gate_att(L, g, part):
                need(sp, "x_att", G * (NG * L + g) - (1 - part))
                lo, n = ((0, G - 1), (G - 1, 1))[part]
                sp.dma_start(g_att[:, lo:lo + n, :],
                             gate_rows(L, 0, g, lo, n).partition_broadcast(P)).then_inc(s[f"g_att_ld{part}"], 16)

            def load_gate_mlp(L, g):
                need(sp, "x_mlp", G * (NG * L + g))
                sp.dma_start(g_mlp[:, :, :],
                             gate_rows(L, 1, g, 0, G).partition_broadcast(P)).then_inc(s["g_mlp_ld"], 16)

            def store_gates(L):
                need(sp, "gate_c", 2 * L + 2)
                sp.dma_start(gate_dram[L].rearrange("w b c -> b w c"),
                             gates[:, L, :].rearrange("b (w c) -> b w c", w=2)).then_inc(s["gate_st"], 16)
                need(sp, "gate_st", 16 * (L + 1))

            def attention(what, i, L, g, start=False):
                a = NG * L + g
                if what == "GATE_LOAD":
                    if start and L == 0:
                        store_gates(0)
                    load_gate_att(L, g, i)
                if what == "MOD":
                    if i in (0, 3):
                        load_late(1 if i == 0 else 2)
                    if i == MOD_STEPS - 1:
                        store_gates(1)
                if L == 0 and what == "NORM_APPLY" and isinstance(g, int) and g == NG - 1:
                    load_late(0)
                if L == 0 and what == "GATE_LOAD" and i == 1 and isinstance(g, int) and g == NG - 1:
                    load_late(3)
                nxt = a if start else a + 1
                if what == "QK_PARTS":
                    store_parts(nxt, i)
                if what == "LOAD":
                    load_qk(a + i[0], i[1])

            def mlp(what, i, L, g):
                m = NG * L + g
                if what == "GATE_LOAD":
                    load_gate_mlp(L, g)
                if what == "DOWN" and i == G - 1 and L == 1:
                    need(sp, "x_mlp", G * m + G)
                    t = G * g
                    ov = out.rearrange("b p c -> p b c")
                    dst = ov[:, t:t + G, :] if isinstance(g, int) else ov[:, bass.ds(t, G), :]
                    src = xs[:, t * C:(t + G) * C] if isinstance(g, int) \
                        else xs[:, bass.ds(t * C, G * C)]
                    sp.dma_start(dst, src.rearrange("p (b c) -> p b c", c=C)).then_inc(s["st_out"], 16)

            phases(sp, lambda: None, attention, mlp)
            sp.wait_ge(s["st_out"], 16 * NG)

        @block.gpsimd
        def _(pool):
            gp = nc.gpsimd
            gp.memset(ident[:, :], 0.0)
            gp.memset(identb[:, :], 0.0)
            gp.memset(xr[:, :, :, :], 0.0)
            gp.memset(minus_half[:, :], -0.5)
            gp.memset(lnr[:, 0:1], 1.0)
            gp.memset(lnr[:, 1:2], 0.0)
            gp.memset(lnr[:, 2:3], 1.0)
            gp.memset(lnr[:, 3:4], 0.0).then_inc(s["pooled"], 1)
            pool.wait_ge(s["pooled"], 1)
            for m in (ident, identb):
                gp.affine_select(out=m[:, :], in_=m[:, :], compare_op=ALU.not_equal, fill=1.0, base=0,
                                 pattern=[[-1, P]], channel_multiplier=1)
            gp.memset(xr[:, :, :, CR:CR + 1], 1.0).then_inc(s["pooled"], 1)
            gp.memset(V[:, :, :, :], 0.0).then_inc(s["pooled"], 1)
            pool.wait_ge(s["pooled"], 3)
            gp.memset(V[:, :, :, HD:HD + 1], 1.0)
            gp.memset(sgr[:, :], 0.0)
            gp.memset(beat[:, :, :, :], 0.0)
            gp.memset(s1r, 0.0)
            gp.memset(sfr, 0.0)
            gp.memset(w2_sb[:, MT1 - 1:MT1 + 1, :], 0.0)
            gp.memset(w2_sb[:, 3 * MT1 - 1:3 * MT1 + 1, :], 0.0)
            gp.memset(an[:, C:C + 1], 1.0).then_inc(s["pooled"], 1)

            def split(n, hi, lo, rest, src, srcr):
                gp.tensor_tensor(lo[:, :], src, hi[:, :].bitcast(F32),
                                 ALU.subtract).then_inc(s["split_s"], 1)
                pool.wait_ge(s["split_s"], 3 * n + 1)
                for i in range(2):
                    a = SLOT * (2 * i + 1)
                    gp.tensor_tensor(rest[a:a + SLOT, :], srcr[a:a + SLOT, :],
                                     rest[a:a + SLOT, :].bitcast(F32),
                                     ALU.subtract).then_inc(s["split_s"], 1)
                    pool.wait_ge(s["split_s"], 3 * n + 2 + i)

            def inverse_deviation(ph, g):
                n = NG * ph + g
                need(pool, "aggr_s", n + 1)
                gp.tensor_tensor(rstd[:, :], var_eps[:, :], minus_half[:, :],
                                 ALU.pow).then_inc(s["rstd_s"], 1)

            def part_c(a, t):
                n = rows(t)
                need(pool, "part_b", 3 * a + t + 1)
                gp.tensor_tensor(parts[0:n, t, 2, :], resid[0:n, :], parts[0:n, t, 1, :],
                                 ALU.subtract).then_inc(s["part_c"], 1)

            def attention(what, i, L, g, start=False):
                a = NG * L + g
                if what == "NORM":
                    inverse_deviation(*after(2 * L, g))
                if what == "QK_PARTS":
                    part_c(a if start else a + 1, i)
                if L == 0 and isinstance(g, int) and g == NG - 1 \
                        and (what == "H_SPLIT" or what == "GATE_LOAD" and i == 1):
                    pool.wait_ge(s["wsplit"], 2 if what == "H_SPLIT" else 3)
                    if what == "H_SPLIT":
                        split(0, w1_hi, w1_lo, w1_r, s1, s1r)
                    else:
                        split(1, wg_hi, wg_lo, wg_r, sg[:, :], sgr[:, :])
                        split(2, f1_hi, f1_lo, f1_r, sf, sfr)

            def mlp(what, i, L, g):
                if what == "NORM":
                    inverse_deviation(*after(2 * L + 1, g))
                if what != "MIX":
                    return
                if isinstance(g, int) and g == 0:
                    pool.wait_ge(s["ld_w2"], NW2)
                for j in range(G):
                    t = G * g + j
                    if j == 0:
                        need(pool, "cw_s", g + 1)
                    wcol = cw[:, j, :].unsqueeze(2).to_broadcast([P, EXPERTS, C])
                    need(pool, "b2_s", 3 * t - 1)
                    gp.tensor_tensor(bw[:, :, :], b2_sb[:, :, :], wcol, ALU.mult).then_inc(s["b2_s"], 1)
                    need(pool, "b2_s", 3 * t + 1)
                    gp.tensor_tensor(bw2[:, :, :], bw[:, 0:2, :], bw[:, 2:4, :],
                                     ALU.add).then_inc(s["b2_s"], 1)
                    need(pool, "b2_s", 3 * t + 2)
                    need(pool, "acc_s", 4 * (t - 2) + 1)
                    gp.tensor_tensor(bias2[:, j % 2, :], bw2[:, 0, :], bw2[:, 1, :],
                                     ALU.add).then_inc(s["b2_s"], 1)

            def setup():
                inverse_deviation(0, 0)
                pool.wait_ge(s["pooled"], 4)
                pool.wait_ge(s["rstd_s"], 1)
                gp.memset(KA[64:96, :, :, :], -1.0).then_inc(s["pooled"], 1)
                pool.wait_ge(s["pooled"], 5)

            phases(pool, setup, attention, mlp)

        @block.scalar
        def _(act):
            sc = nc.scalar

            def h_main(ph, g):
                n = NG * ph + g
                inputs_used(act, ph, g)
                if isinstance(n, int) and n == 0:
                    act.wait_ge(s["mod_read"], 1)
                need(act, "T_done", 2 * n + 1)
                for j in range(G):
                    t = G * g + j
                    last = sc.activation(h32[:, j * SEQ:(j + 1) * SEQ], PREP[:, j * SEQ:(j + 1) * SEQ],
                                         ACT.Identity, bias=col(b_main, ph, t), scale=col(a_main, ph, t))
                last.then_inc(s["h_main"], 1)

            def h_round(ph, g, rest):
                n = NG * ph + g
                if rest:
                    need(act, "h_rest", n + 1)
                    sc.copy(hR[:, :], r32[:, :]).then_inc(s["r_hi"], 1)
                else:
                    need(act, "h_main", n + 1)
                    sc.copy(hhi[:, :], h32[:, :]).then_inc(s["h_hi"], 1)

            def part_a(a, t, src):
                n = rows(t)
                if t == 0:
                    need(act, "scr_w", 192 * a)
                need(act, "qk_mm", 3 * a + t + 1)
                sc.copy(parts[0:n, t, 0, :], src[0:n, :]).then_inc(s["part_a"], 1)

            def part_b(a, t):
                n = rows(t)
                need(act, "part_r", 3 * a + t + 1)
                sc.copy(parts[0:n, t, 1, :], resid[0:n, :]).then_inc(s["part_b"], 1)

            def v_out(a, k):
                need(act, "v_mm", 2 * a + k + 1)
                if isinstance(a, int) and a == 0 and k == 0:
                    act.wait_ge(s["pooled"], 4)
                if k == 0:
                    need(act, "pv_mm", 16 * (a - 1) + 12)
                    sc.copy(V[:, 0:G - 1, :, 0:HD].rearrange("p j h d -> p (j h) d"),
                            PREP[:, 0:(G - 1) * C].rearrange("p (h d) -> p h d", d=HD)
                            ).then_inc(s["v_ready"], 1)
                else:
                    need(act, "v3_ready", a)
                    sc.copy(v_last[:, :], SMALL[:, 0:C]).then_inc(s["v_ready"], 1)

            def v_take(a):
                need(act, "v_ready", 2 * a + 2)
                need(act, "pv_mm", 16 * a)
                sc.copy(V[:, G - 1, :, 0:HD],
                        v_last[:, :].rearrange("p (h d) -> p h d", d=HD)).then_inc(s["v3_ready"], 1)

            def m_out(B):
                need(act, "mt_mm", B + 1)
                need(act, "m_ld", 16 * B)
                sc.copy(mT[:, :], SMALL[0:2 * HEADS, 0:SEQ // 2].bitcast(BF16)).then_inc(s["mt_c"], 1)

            def m_store(B, j):
                need(act, "mt_c", B + 1)
                act.dma_start(QA[SROWS:MROWS, j, :, :], mT[:, :]).then_inc(s["m_ld"], 16)

            def exp_quad(qi, q):
                need(act, "st_mm", qi + 1)
                need(act, "pv_mm", qi - 1)
                sc.activation(pr[:, q % 2, :], bank[ST_BANK[q % 2]][:, :], ACT.Exp,
                              scale=SCALE).then_inc(s["exp_s"], 1)

            def o_out(B, j):
                need(act, "pv_mm", 4 * B + 4)
                need(act, "o_T", B)
                sc.copy(osb[:, :], bank[O_BANK[j % 2]][:, :]).then_inc(s["o_ev"], 1)

            def a_out(B, o_bank):
                need(act, "a_T", B + 1)
                need(act, "proj_mm", B)
                sc.copy(aT[:, :], o_bank[:, 0:SEQ])
                sc.copy(aTr[:, :], o_bank[0:CR + 1, SEQ:2 * SEQ]).then_inc(s["a_c"], 1)

            def gates_out(L):
                act.wait_ge(s["mod_mm"], 3 * L + 3)
                if L == 1:
                    act.wait_ge(s["mod_read"], 2)
                for w in range(2):
                    sc.copy(gates[:, L, w * C:(w + 1) * C],
                            GATE_BANK[L][0:BATCH, w * C:(w + 1) * C]).then_inc(s["gate_c"], 1)

            def setup():
                act.wait_ge(s["ld_c"], 16)
                sc.activation(c_tmp[:, C:2 * C], c_nat[:, 0:C], ACT.Exp, scale=-1.0).then_inc(s["silu"], 1)
                act.wait_ge(s["cond_T"], 1)
                sc.copy(cT[:, :], SMALL[:, 0:BATCH])
                sc.copy(cTr[:, :], SMALL[0:CR + 1, BATCH:2 * BATCH]).then_inc(s["cond_c"], 1)

            def attention(what, i, L, g, start=False):
                a = NG * L + g
                nxt = a if start else a + 1
                if what == "SCORE":
                    exp_quad(16 * a + i, i % 2)
                if what == "PV" and i % QUADS == QUADS - 1:
                    o_out(G * a + i // QUADS, i // QUADS)
                if what == "MAX_STORE":
                    m_store(G * a + i, i % G)
                if what == "MAX_T":
                    m_out(G * a + i)
                if what == "ATT_T":
                    a_out(G * a + i, bank[O_BANK[i % 2]])
                if what == "V":
                    v_out(a + i[0], i[1])
                if what == "V3":
                    v_take(a)
                if what == "H_MAIN":
                    h_main(*after(2 * L, g))
                if what in ("H_REST", "H_SPLIT"):
                    h_round(*after(2 * L, g), what == "H_SPLIT")
                if what == "QK":
                    part_a(nxt, i, START_BANK[i] if start else PREP)
                if what == "QK_PARTS":
                    part_b(nxt, i)
                if what == "MOD" and i == MOD_STEPS - 1:
                    gates_out(1)
                if L == 0 and isinstance(g, int) and g == NG - 1:
                    if what == "NORM":
                        act.wait_ge(s["ld_w1"], 16 * (2 + 3 * NS))
                        sc.copy(w1_hi[:, :], s1).then_inc(s["wsplit"], 1)
                    if what == "H_SPLIT":
                        sc.copy(w1_r[:, :], s1r).then_inc(s["wsplit"], 1)
                    if what == "GATE_LOAD" and i == 1:
                        act.wait_ge(s["ld_f1"], 16 * (1 + 2 * NS))
                        for dst, src in ((wg_hi[:, :], sg[:, :]), (wg_r[:, :], sgr[:, :]),
                                         (f1_hi[:, :], sf), (f1_r[:, :], sfr)):
                            last = sc.copy(dst, src)
                        last.then_inc(s["wsplit"], 1)

            def mlp(what, i, L, g):
                if what == "LOGITS":
                    need(act, "gl_mm", g + 1)
                    need(act, "lg_T", g)
                    sc.copy(lgT[:, :], SMALL[0:EXPERTS, :]).then_inc(s["gl_c"], 1)
                if what == "UP" and L == 0:
                    if i == 0 and isinstance(g, int) and g == 0:
                        act.wait_ge(s["split_s"], 9)
                    if i == 0:
                        need(act, "w2_mm", 8 * g)
                    need(act, "w1_mm", MT0 * g + i + 1)
                    sc.activation(hid[:, i * GT:(i + 1) * GT], bank[i % 4][:, :],
                                  ACT.Gelu_apprx_tanh).then_inc(s["gelu"], 1)
                if what == "UP" and L == 1:
                    if i == 0:
                        need(act, "w2_mm", 8 * NG)
                        need(act, "f2_mm", G * g)
                    need(act, "f1_mm", MT1 * g + i + 1)
                    n = P if i < 4 else HID - 4 * P
                    dst = hid[:, i * GT:(i + 1) * GT] if i < 4 else hid4[0:n, :]
                    sc.activation(dst, bank[i % 4][0:n, :], ACT.Gelu).then_inc(s["f1_gelu"], 1)
                if what == "MIX":
                    need(act, "gate_e", g + 1)
                    sc.activation(ex[:, :, :], dl[:, :, :], ACT.Exp).then_inc(s["gate_x"], 1)
                if what == "H_MAIN":
                    h_main(*after(2 * L + 1, g))
                if what in ("H_REST", "H_SPLIT"):
                    h_round(*after(2 * L + 1, g), what == "H_SPLIT")

            def start():
                setup()
                h_main(0, 0)
                h_round(0, 0, False)
                h_round(0, 0, True)
                gates_out(0)

            phases(act, start, attention, mlp)

        @block.vector
        def _(dve):
            v = nc.vector
            done = [0]

            def step(ins):
                done[0] += 1
                ins.then_inc(s["mod_done"], 1)
                dve.wait_ge(s["mod_done"], done[0])

            def weights(L):
                dve.wait_ge(s["ld_qkv%d" % L], NQKV[L])
                for src, dst in ((sq[L], wp32), (sqr[L], wr32)):
                    sv = src[:, 0:2 * C].rearrange("p (w h d) -> p w d h", w=2, d=HD)
                    for w in range(2):
                        v.tensor_copy(dst[:, w * ROWS8:(w + 1) * ROWS8].rearrange("p (d h) -> p d h", d=8),
                                      sv[:, w, 0:8, :])
                    last = v.tensor_copy(dst[:, 2 * ROWS8:2 * C].rearrange("p (w h) -> p w h", w=2),
                                         sv[:, :, 8, :])
                step(last)
                v.tensor_copy(wqk_hi[L][:, :], wp32[:, :])
                v.tensor_copy(wqk_r[L][:, :], wr32[:, :])
                step(v.tensor_copy(wv_r[L][:, :], sqr[L][:, 2 * C:3 * C]))
                v.tensor_tensor(wqk_lo[L][:, :], wp32[:, :], wqk_hi[L][:, :].bitcast(F32), ALU.subtract)
                for k in (1, 3):
                    a, b = SLOT * k, SLOT * (k + 1)
                    v.tensor_tensor(wqk_r[L][a:b, :], wr32[a:b, :], wqk_r[L][a:b, :].bitcast(F32),
                                    ALU.subtract)
                    last = v.tensor_tensor(wv_r[L][a:b, :], sqr[L][a:b, 2 * C:3 * C],
                                           wv_r[L][a:b, :].bitcast(F32), ALU.subtract)
                last.then_inc(s["qk_weights"], 1)
                dve.wait_ge(s["qk_weights"], L + 1)

            def modulation(L):
                dve.wait_ge(s["mod_mm"], 1 if L == 0 else 6)
                if L == 1:
                    dve.wait_ge(s["ld_ln"], NLN)
                bk = MOD_BANK[L]
                for i in range(2):
                    ph = 2 * L + i
                    sh, scl = bk[:, 32 * i:32 * i + 16], bk[:, 32 * i + 16:32 * i + 32]
                    shr, sclr = bk[:, 64 + 32 * i:80 + 32 * i], bk[:, 80 + 32 * i:96 + 32 * i]
                    v.tensor_scalar(a_main[:, ph, :], scl, 1.0, None, ALU.add)
                    v.tensor_copy(b_main[:, ph, :], sh)
                    v.tensor_scalar(a_rest[:, ph, :], sclr, mask[:, 0:1], mask[:, 1:2], ALU.mult, ALU.add)
                    step(v.tensor_scalar(b_rest[:, ph, :], shr, mask[:, 0:1], None, ALU.mult))
                    if L == 1:
                        for a, b, ln in ((a_main, b_main, lnm), (a_rest, b_rest, lnr)):
                            step(v.scalar_tensor_tensor(b[:, ph, :], a[:, ph, :], ln[:, 2 * i + 1:2 * i + 2],
                                                        b[:, ph, :], ALU.mult, ALU.add))
                            step(v.tensor_scalar(a[:, ph, :], a[:, ph, :], ln[:, 2 * i:2 * i + 1], None,
                                                 ALU.mult))
                v.memset(c_tmp[:, 0:1], 0.0).then_inc(s["mod_read"], 1)

            def norm(ph, g):
                n = NG * ph + g
                if ph == 0:
                    if isinstance(g, int) and g == 0:
                        dve.wait_ge(s["ld_x0"], 16)
                    else:
                        dve.wait_ge(s["ld_x"], 16)
                elif ph == 2:
                    need(dve, "x_mlp", G * g + G)
                else:
                    need(dve, "x_att", BATCH * (ph // 2) + G * g + G)
                need(dve, "normed", n)
                for j in range(G):
                    last = v.bn_stats(stats[:, j, :], xt(G * g + j))
                last.then_inc(s["stats_s"], 1)
                need(dve, "stats_s", n + 1)
                even, odd = stats[:, :, 0:3], stats[:, :, 3:6]
                v.tensor_tensor(msum[:, :], even[:, :, 1], odd[:, :, 1], ALU.add)
                v.tensor_tensor(mdif[:, :], even[:, :, 1], odd[:, :, 1], ALU.subtract)
                v.tensor_tensor(sq2[:, :], even[:, :, 2], odd[:, :, 2], ALU.add).then_inc(s["sums_s"], 1)
                need(dve, "sums_s", n + 1)
                v.tensor_scalar(mean[:, :], msum[:, :], 0.5, None, ALU.mult)
                v.scalar_tensor_tensor(vdif[:, :], mdif[:, :], 0.25, mdif[:, :], ALU.mult, ALU.mult)
                v.tensor_scalar(vown[:, :], sq2[:, :], 1.0 / C, EPS[ph // 2], ALU.mult,
                                ALU.add).then_inc(s["vars_s"], 1)
                need(dve, "vars_s", n + 1)
                v.tensor_tensor(var_eps[:, :], vdif[:, :], vown[:, :], ALU.add).then_inc(s["aggr_s"], 1)

            def norm_apply(ph, g):
                n = NG * ph + g
                need(dve, "rstd_s", n + 1)
                need(dve, "T_done", 2 * n)
                if isinstance(n, int) and n == 0:
                    dve.wait_ge(s["pooled"], 2)
                for j in range(G):
                    x_ = xt(G * g + j)
                    v.tensor_scalar(xn[:, j, :], x_[:, 0:CM], mean[:, j:j + 1], rstd[:, j:j + 1],
                                    ALU.subtract, ALU.mult)
                    last = v.tensor_scalar(xr[:, j, :, 0:CR],
                                           x_[:, CM:C].unsqueeze(1).to_broadcast([P, NS, CR]),
                                           mean[:, j:j + 1], rstd[:, j:j + 1], ALU.subtract, ALU.mult)
                last.then_inc(s["normed"], 1)

            def h_rest(ph, g):
                n = NG * ph + g
                need(dve, "T_done", 2 * n + 2)
                inputs_used(dve, ph, g)
                for j in range(G):
                    t = G * g + j
                    last = v.tensor_scalar(r32[:, j * SEQ:(j + 1) * SEQ], PREP[:, j * SEQ:(j + 1) * SEQ],
                                           col(a_rest, ph, t), col(b_rest, ph, t), ALU.mult, ALU.add)
                last.then_inc(s["h_rest"], 1)

            def h_split(ph, g):
                n = NG * ph + g
                need(dve, "h_hi", n + 1)
                v.tensor_tensor(hlo[:, :], h32[:, :], hhi[:, :].bitcast(F32), ALU.subtract)
                need(dve, "r_hi", n + 1)
                half = slice(2 * SLOT, P)
                v.tensor_tensor(hR[half, :], r32[half, :], hR[half, :].bitcast(F32),
                                ALU.subtract).then_inc(s["h_ready"], 1)

            def part_r(a, t, src):
                n = rows(t)
                need(dve, "part_a", 3 * a + t + 1)
                need(dve, "part_c", 3 * a + t)
                v.tensor_tensor(resid[0:n, :], src[0:n, :], parts[0:n, t, 0, :],
                                ALU.subtract).then_inc(s["part_r"], 1)

            def row_max(B, q):
                need(dve, "s_mm", 4 * B + q + 1)
                if q == 0:
                    need(dve, "msplit", 2 * B)
                v.tensor_reduce(mx[:, HQ * q:HQ * (q + 1)],
                                bank[S_BANK[q % 2]][:, :].rearrange("p (h k) -> p h k", k=SEQ),
                                AX.X, ALU.max).then_inc(s["max_s"], 1)

            def max_split(B):
                need(dve, "max_s", 4 * B + 4)
                need(dve, "mt_mm", B)
                v.tensor_copy(mp[:, 0, :], mx[:, :]).then_inc(s["msplit"], 1)
                need(dve, "msplit", 2 * B + 1)
                v.tensor_tensor(mp[:, 1, :], mx[:, :], mp[:, 0, :], ALU.subtract).then_inc(s["msplit"], 1)
                need(dve, "msplit", 2 * B + 2)

            def normalise(B, o_bank):
                need(dve, "o_T", B + 1)
                ov = o_bank[:, :].rearrange("p (h w) -> p h w", w=VW)
                v.reciprocal(rinv[:, :], ov[:, :, HD]).then_inc(s["rinv_s"], 1)
                need(dve, "rinv_s", B + 1)
                need(dve, "a_T", B)
                v.tensor_tensor(an[:, 0:C].rearrange("p (h d) -> p h d", d=HD), ov[:, :, 0:HD],
                                rinv[:, :].unsqueeze(2).to_broadcast([P, HEADS, HD]),
                                ALU.mult).then_inc(s["an_s"], 1)
                need(dve, "an_s", B + 1)

            def attention_residual(a, t, B, j, o_bank):
                need(dve, "proj_mm", B + 1)
                if j in (0, G - 1):
                    need(dve, "g_att_ld0" if j == 0 else "g_att_ld1", 16 * (a + 1))
                v.tensor_tensor(tmp[:, :], o_bank[:, 0:C], g_att[:, j, :], ALU.mult).then_inc(s["att_t"], 1)
                need(dve, "att_t", B + 1)
                v.tensor_tensor(xt(t), xt(t), tmp[:, :], ALU.add).then_inc(s["x_att"], 1)

            def gating(g):
                n = 4 * g
                need(dve, "lg_T", g + 1)
                need(dve, "cw_b", g)
                v.tensor_copy(lg[:, :, :].rearrange("p j e -> p (j e)"),
                              SMALL[:, 0:G * EXPERTS]).then_inc(s["gate_s"], 1)
                need(dve, "gate_s", n + 1)
                v.tensor_reduce(lmax[:, :], lg[:, :, :], AX.X, ALU.max)
                for e in range(EXPERTS):
                    for lo, hi, op in ((0, e, ALU.is_gt), (e + 1, EXPERTS, ALU.is_ge)):
                        if lo < hi:
                            last = v.tensor_tensor(beat[:, e, :, lo:hi],
                                                   lg[:, :, e:e + 1].to_broadcast([P, G, hi - lo]),
                                                   lg[:, :, lo:hi], op)
                last.then_inc(s["gate_s"], 1)
                need(dve, "gate_s", n + 2)
                v.tensor_tensor(dl[:, :, :], lg[:, :, :],
                                lmax[:, :].unsqueeze(2).to_broadcast([P, G, EXPERTS]),
                                ALU.subtract).then_inc(s["gate_e"], 1)
                v.tensor_reduce(cnt[:, :, :], beat[:, :, :, :].rearrange("p b j e -> p j e b"),
                                AX.X, ALU.add).then_inc(s["gate_s"], 1)
                need(dve, "gate_s", n + 3)
                v.tensor_scalar(sel[:, :, :], cnt[:, :, :], 1.5, None, ALU.is_lt).then_inc(s["gate_s"], 1)
                need(dve, "gate_s", n + 4)

            def mixing(g):
                need(dve, "gate_x", g + 1)
                v.tensor_tensor(es[:, :, :], ex[:, :, :], sel[:, :, :], ALU.mult).then_inc(s["cw_b"], 1)
                need(dve, "cw_b", g + 1)
                v.tensor_reduce(den[:, :], es[:, :, :], AX.X, ALU.add).then_inc(s["mix_s"], 1)
                need(dve, "mix_s", 2 * g + 1)
                v.reciprocal(rden[:, :], den[:, :]).then_inc(s["mix_s"], 1)
                need(dve, "mix_s", 2 * g + 2)
                need(dve, "b2_s", 12 * g)
                v.tensor_tensor(cw[:, :, :], es[:, :, :],
                                rden[:, :].unsqueeze(2).to_broadcast([P, G, EXPERTS]),
                                ALU.mult).then_inc(s["cw_s"], 1)

            def experts_residual(g, j, pair):
                t = G * g + j
                if j == 0 and pair == 0:
                    need(dve, "cw_s", g + 1)
                    need(dve, "g_mlp_ld", 16 * (g + 1))
                if pair == 0:
                    need(dve, "b2_s", 3 * t + 3)
                for e in (2 * pair, 2 * pair + 1):
                    if e % 2 == 0:
                        need(dve, "w2_mm", 2 * t + e // 2 + 1)
                    need(dve, "acc_s", 4 * t + e)
                    src = bank[O_BANK[e // 2]][:, (e % 2) * C:(e % 2 + 1) * C]
                    v.scalar_tensor_tensor(acc[:, :], src, cw[:, j, e:e + 1],
                                           bias2[:, j % 2, :] if e == 0 else acc[:, :],
                                           ALU.mult, ALU.add).then_inc(s["acc_s"], 1)
                if pair == 0:
                    return
                need(dve, "acc_s", 4 * t + 4)
                v.tensor_tensor(tmp[:, :], acc[:, :], g_mlp[:, j, :], ALU.mult).then_inc(s["acc_g"], 1)
                need(dve, "acc_g", t + 1)
                v.tensor_tensor(xt(t), xt(t), tmp[:, :], ALU.add).then_inc(s["x_mlp"], 1)

            def mlp_residual(g, j):
                t = G * g + j
                if j == 0:
                    need(dve, "g_mlp_ld", 16 * (NG + g + 1))
                need(dve, *(("x_att", 2 * BATCH) if isinstance(t, int) and t == 0
                            else ("x_mlp", BATCH + t)))
                need(dve, "f2_mm", t + 1)
                v.tensor_tensor(tmp[:, :], bank[O_BANK[j % 2]][:, 0:C], g_mlp[:, j, :],
                                ALU.mult).then_inc(s["f2_t"], 1)
                need(dve, "f2_t", t + 1)
                v.tensor_tensor(xt(t), xt(t), tmp[:, :], ALU.add).then_inc(s["x_mlp"], 1)

            def setup():
                v.memset(sqr[0][:, :], 0.0)
                v.memset(sqr[1][:, :], 0.0).then_inc(s["zeroed"], 1)
                v.memset(c_nat[:, C:C + 1], 1.0)
                step(v.memset(mask[:, :], 0.0))
                for k in range(NS):
                    v.memset(mask[SLOT * k:SLOT * k + CR, 0:1], 1.0)
                    v.memset(mask[SLOT * k:SLOT * k + CR + 1, 1:2], 1.0)
                dve.wait_ge(s["silu"], 1)
                step(v.tensor_scalar(c_tmp[:, 0:C], c_tmp[:, C:2 * C], 1.0, None, ALU.add))
                step(v.reciprocal(c_tmp[:, 2 * C:3 * C], c_tmp[:, 0:C]))
                v.tensor_tensor(c_nat[:, 0:C], c_nat[:, 0:C], c_tmp[:, 2 * C:3 * C],
                                ALU.mult).then_inc(s["silu"], 1)
                norm(0, 0)
                norm_apply(0, 0)
                modulation(0)
                weights(0)
                v.memset(hid4[64:65, :], 1.0)
                h_rest(0, 0)
                h_split(0, 0)

            def attention(what, i, L, g, start=False):
                a = NG * L + g
                B = G * a
                if what == "NORM":
                    norm(*after(2 * L, g))
                if what == "NORM_APPLY":
                    norm_apply(*after(2 * L, g))
                if what == "H_REST":
                    h_rest(*after(2 * L, g))
                if what == "H_SPLIT":
                    h_split(*after(2 * L, g))
                if what == "QK":
                    part_r(a if start else a + 1, i, START_BANK[i] if start else PREP)
                if what == "MAX":
                    row_max(B + i // QUADS, i % QUADS)
                    if i % QUADS == QUADS - 1:
                        max_split(B + i // QUADS)
                if what == "MOD" and i == MOD_STEPS - 1:
                    modulation(1)
                if L == 0 and what == "MAX_T" and i == G - 1 and isinstance(g, int) and g == NG - 1:
                    weights(1)
                if what == "OUT_T":
                    normalise(B + i, bank[O_BANK[i % 2]])
                if what == "PROJ":
                    attention_residual(a + i // G, G * g + i, B + i, i % G, bank[O_BANK[i % 2]])

            def mlp(what, i, L, g):
                if what == "NORM":
                    norm(*after(2 * L + 1, g))
                if what == "NORM_APPLY":
                    norm_apply(*after(2 * L + 1, g))
                if what == "H_REST":
                    h_rest(*after(2 * L + 1, g))
                if what == "H_SPLIT":
                    h_split(*after(2 * L + 1, g))
                if what == "LOGITS_T":
                    gating(g)
                if what == "MIX":
                    mixing(g)
                if what == "DOWN":
                    if L == 0:
                        experts_residual(g, i // 2, i % 2)
                    else:
                        mlp_residual(g, i)

            phases(dve, setup, attention, mlp)

        @block.tensor
        def _(pe):
            te = nc.tensor

            def transposes(ph, g, rest):
                n = NG * ph + g
                if rest:
                    need(pe, "h_main", n + 1)
                else:
                    need(pe, "normed", n + 1)
                    need(pe, "h_rest", n)
                for j in range(G):
                    src = xr[:, j, :, :].rearrange("p s c -> p (s c)") if rest else xn[:, j, :]
                    last = te.transpose(PREP[:, j * SEQ:(j + 1) * SEQ], src, ident[:, :])
                last.then_inc(s["T_done"], 1)

            def product(dst, hi, lo, rest, cols):
                te.matmul(dst, lo[:, cols], hhi[:, :], start=True, stop=False)
                te.matmul(dst, hi[:, cols], hlo[:, :], start=False, stop=False)
                te.matmul(dst, rest[:, cols], hR[:, :], start=False, stop=False)
                return te.matmul(dst, hi[:, cols], hhi[:, :], start=False, stop=True)

            def qk(ph, g, a, L, t, dst):
                if t == 0:
                    need(pe, "h_ready", NG * ph + g + 1)
                    need(pe, "qk_weights", L + 1)
                if dst is PREP:
                    need(pe, "part_r", 3 * a + t)
                cols = slice((t - 1) * ROWS8, t * ROWS8) if t > 0 else slice(2 * ROWS8, 2 * C)
                product(dst[0:rows(t), :], wqk_hi[L], wqk_lo[L], wqk_r[L], cols).then_inc(s["qk_mm"], 1)

            def values(a, L, k):
                if k == 0:
                    need(pe, "part_r", 3 * a + 3)
                else:
                    need(pe, "mt_c", G * a)
                for c, j in enumerate(((0, 1, 2), (3,))[k]):
                    dst, tok = (PREP, SMALL)[k][:, c * C:(c + 1) * C], slice(j * SEQ, (j + 1) * SEQ)
                    te.matmul(dst, h32[:, tok], sq[L][:, 2 * C:3 * C], start=True, stop=False)
                    last = te.matmul(dst, hR[:, tok], wv_r[L][:, :], start=False, stop=True)
                last.then_inc(s["v_mm"], 1)

            def scores(a, B, j, q):
                qi = 4 * B + q
                need(pe, "max_s", qi - 1)
                if q == 0:
                    pe.wait_ge(qk_ld[j], QK_LOADS * (a + 1))
                for i in range(HQ):
                    h = HQ * q + i
                    last = te.matmul(bank[S_BANK[q % 2]][:, i * SEQ:(i + 1) * SEQ],
                                     QA[0:SROWS, j, h, :], KA[0:SROWS, j, h, :], start=True, stop=True)
                last.then_inc(s["s_mm"], 1)

            def scores_T(B, j, q):
                need(pe, "exp_s", 4 * B + q - 1)
                if q == 0:
                    need(pe, "m_ld", 16 * (B + 1))
                for i in range(HQ):
                    h = HQ * q + i
                    last = te.matmul(bank[ST_BANK[q % 2]][:, i * SEQ:(i + 1) * SEQ],
                                     KA[0:MROWS, j, h, :], QA[0:MROWS, j, h, :], start=True, stop=True)
                last.then_inc(s["st_mm"], 1)

            def weigh(a, B, j, q):
                need(pe, "exp_s", 4 * B + q + 1)
                if q == 0:
                    need(pe, "att_t", B - 1)
                    need(pe, *(("v3_ready", a + 1) if j == G - 1 else ("v_ready", 2 * a + 1)))
                for i in range(HQ):
                    last = te.matmul(bank[O_BANK[j % 2]][SLOT * i:SLOT * (i + 1), q * SEQ:(q + 1) * SEQ],
                                     V[:, j, HQ * q + i, :], pr[:, q % 2, i * SEQ:(i + 1) * SEQ],
                                     start=True, stop=True)
                last.then_inc(s["pv_mm"], 1)

            def out_T(B, o_bank):
                need(pe, "o_ev", B + 1)
                for q in range(QUADS):
                    last = te.transpose(o_bank[:, q * SEQ:(q + 1) * SEQ], osb[:, q * SEQ:(q + 1) * SEQ],
                                        ident[:, :])
                last.then_inc(s["o_T"], 1)

            def max_T(B):
                need(pe, "msplit", 2 * B + 2)
                need(pe, "mt_c", B)
                te.transpose(SMALL[0:2 * HEADS, 0:SEQ // 2].bitcast(BF16),
                             mp[:, :, :].rearrange("p s h -> p (s h)"), identb[:, :]).then_inc(s["mt_mm"], 1)

            def att_T(B, o_bank):
                need(pe, "an_s", B + 1)
                te.transpose(o_bank[:, 0:SEQ], an[:, 0:CM], ident[:, :])
                te.transpose(o_bank[0:CR + 1, SEQ:2 * SEQ], an[:, CM:C + 1], ident[:, :]).then_inc(s["a_T"], 1)

            def project(L, B, o_bank):
                need(pe, "a_c", B + 1)
                te.matmul(o_bank[:, 0:C], aTr[:, :], wo_r[L][:, :], start=True, stop=False)
                te.matmul(o_bank[:, 0:C], aT[:, :], wo_m[L][:, :], start=False,
                          stop=True).then_inc(s["proj_mm"], 1)

            def modulation(L, steps):
                pe.wait_ge(s[f"ld_ada{L}"], NADA)
                bk = MOD_BANK[L]

                def modulate(dst, lo, n):
                    te.matmul(dst, ada_m[L][:, lo:lo + n], cT[:, :], start=True, stop=False)
                    return te.matmul(dst, ada_r[L][:, lo:lo + n], cTr[:, :], start=False, stop=True)

                for i in steps:
                    if i < len(MSET):
                        k = MSET[i]
                        modulate(bk[:, 16 * i:16 * i + 16], k * C, CM)
                        for n in range(NS):
                            last = modulate(bk[SLOT * n:SLOT * (n + 1), 64 + 16 * i:80 + 16 * i],
                                            k * C + CM, SLOT)
                        if i == len(MSET) - 1:
                            last.then_inc(s["mod_mm"], 1)
                        continue
                    for w, k in enumerate((2, 5)):
                        dst = GATE_BANK[L][0:BATCH, w * C:(w + 1) * C]
                        te.matmul(dst, cT[:, :], ada_m[L][:, k * C:(k + 1) * C], start=True, stop=False)
                        te.matmul(dst, cTr[:, :], ada_r[L][:, k * C:(k + 1) * C], start=False,
                                  stop=True).then_inc(s["mod_mm"], 1)

            def setup():
                pe.wait_ge(s["pooled"], 2)
                pe.wait_ge(s["silu"], 2)
                te.transpose(SMALL[:, 0:BATCH], c_nat[:, 0:CM], ident[0:BATCH, 0:BATCH])
                te.transpose(SMALL[0:CR + 1, BATCH:2 * BATCH], c_nat[:, CM:C + 1],
                             ident[0:BATCH, 0:BATCH]).then_inc(s["cond_T"], 1)
                pe.wait_ge(s["cond_c"], 1)
                modulation(0, range(4))
                transposes(0, 0, False)
                transposes(0, 0, True)
                modulation(0, (4,))

            def attention(what, i, L, g, start=False):
                a = NG * L + g
                B = G * a
                if L == 1 and start and what == "V":
                    need(pe, "gate_s", 4 * NG)
                if L == 1 and start and what == "MAX" and i == 0:
                    need(pe, "gelu", MT0 * NG)
                if L == 1 and what == "PV" and i == 0 and isinstance(g, int) and g == 0:
                    need(pe, "acc_s", 4 * BATCH)
                if L == 0 and isinstance(g, int) and g == 0 and not start:
                    if what == "PV" and i == 0:
                        need(pe, "gate_c", 2)
                    if what == "PROJ" and i == 0:
                        need(pe, "ld_wo", 16 * 6)
                if what == "H_MAIN":
                    need(pe, "v_ready", 2 * a + 1)
                    transposes(*after(2 * L, g), False)
                if what == "H_REST":
                    transposes(*after(2 * L, g), True)
                if what == "QK":
                    if start:
                        qk(2 * L, g, a, L, i, START_BANK[i])
                    else:
                        qk(2 * L, g + 1, a + 1, L, i, PREP)
                if what == "V":
                    if L == 0 and not start and i == (0, 0):
                        pe.wait_ge(s["mod_read"], 2)
                        pe.wait_ge(s["gate_c"], 4)
                    values(a + i[0], L, i[1])
                if what == "MOD":
                    need(pe, "part_r", 3 * (a + 2))
                    modulation(1, (i,))
                if what == "MAX":
                    scores(a + i // (QUADS * G), B + i // QUADS, i // QUADS % G, i % QUADS)
                if what == "SCORE":
                    scores_T(B + i // QUADS, i // QUADS % G, i % QUADS)
                if what == "PV":
                    weigh(a + i // (QUADS * G), B + i // QUADS, i // QUADS % G, i % QUADS)
                if what == "OUT_T":
                    out_T(B + i, bank[O_BANK[i % 2]])
                if what == "MAX_T":
                    if i == 0:
                        need(pe, "v_ready", 2 * a + 2)
                    max_T(B + i)
                if what == "ATT_T":
                    att_T(B + i, bank[O_BANK[i % 2]])
                if what == "PROJ":
                    project(L, B + i, bank[O_BANK[i % 2]])

            def up(L, g, m):
                count, done, tiles = ("w1_mm", "gelu", MT0) if L == 0 else ("f1_mm", "f1_gelu", MT1)
                if m == 0:
                    need(pe, "h_ready", NG * (2 * L + 1) + g + 1)
                    need(pe, "split_s", 9)
                    need(pe, "exp_s", 64 * (L + 1))
                    need(pe, "max_s", 64 * (L + 1))
                need(pe, done, tiles * g + (m - 3 if m >= 4 else 0))
                n = P if L == 0 or m < 4 else HID - 4 * P
                hi, lo, rest = (w1_hi, w1_lo, w1_r) if L == 0 else (f1_hi, f1_lo, f1_r)
                last = product(bank[m % 4][0:n, :], hi, lo, rest, slice(m * P, m * P + n))
                last.then_inc(s[count], 1)

            def down_experts(g, j, pair):
                t = G * g + j
                tok = slice(j * SEQ, (j + 1) * SEQ)
                if j == 0:
                    need(pe, "gelu", MT0 * g + MT0 // 2 * (pair + 1))
                need(pe, "acc_s", 4 * t - 2 + 2 * pair)
                for e in (2 * pair, 2 * pair + 1):
                    dst = bank[O_BANK[pair]][:, (e % 2) * C:(e % 2 + 1) * C]
                    for i in range(MT1):
                        at = (e * HID // P + i) * GT + j * SEQ
                        last = te.matmul(dst, hid[:, at:at + SEQ], w2_sb[:, MT1 * e + i, :],
                                         start=(i == 0), stop=(i == MT1 - 1))
                last.then_inc(s["w2_mm"], 1)

            def down(g, j):
                t = G * g + j
                if j == 0:
                    need(pe, "f1_gelu", MT1 * (g + 1))
                need(pe, "f2_t", t - 1)
                dst = bank[O_BANK[j % 2]][:, 0:C]
                for m in range(MT1):
                    n = P if m < 4 else HID - 4 * P + 1
                    src = hid[:, m * GT + j * SEQ:m * GT + (j + 1) * SEQ] if m < 4 \
                        else hid4[0:n, j * SEQ:(j + 1) * SEQ]
                    last = te.matmul(dst, src, f2_sb[0:n, m, :], start=(m == 0), stop=(m == MT1 - 1))
                last.then_inc(s["f2_mm"], 1)

            def mlp(what, i, L, g):
                ph = 2 * L + 1
                if what == "LOGITS":
                    need(pe, "h_ready", NG * ph + g + 1)
                    need(pe, "split_s", 9)
                    need(pe, "mt_c", BATCH)
                    need(pe, "gate_s", 4 * g)
                    product(SMALL[0:EXPERTS, :], wg_hi, wg_lo, wg_r,
                            slice(0, EXPERTS)).then_inc(s["gl_mm"], 1)
                if what == "LOGITS_T":
                    for j in range(G):
                        last = te.transpose(SMALL[:, j * EXPERTS:(j + 1) * EXPERTS],
                                            lgT[:, j * SEQ:(j + 1) * SEQ], ident[0:EXPERTS, 0:EXPERTS])
                    last.then_inc(s["lg_T"], 1)
                if what == "UP":
                    if L == 0 and i == 6:
                        need(pe, "gl_c", g + 1)
                    up(L, g, i)
                if what == "DOWN":
                    if isinstance(g, int) and g == 0 and i == 0:
                        pe.wait_ge(s["ld_w2"], NW2)
                        need(pe, "att_t", BATCH * (L + 1))
                    if L == 0:
                        down_experts(g, i // 2, i % 2)
                    else:
                        down(g, i)
                if what == "H_MAIN":
                    transposes(*after(ph, g), False)
                if what == "H_REST":
                    transposes(*after(ph, g), True)

            phases(pe, setup, attention, mlp)


_INS = ["x", "cond_1152",
        "L0_cond_w_adaln", "L0_cond_b_adaln", "L0_cond_w_qkv", "L0_cond_b_qkv", "L0_cond_w_proj",
        "L0_cond_b_proj", "L0_cond_w_gate", "L0_cond_w1", "L0_cond_b1", "L0_cond_w2", "L0_cond_b2",
        "L1_cond_ln1_w", "L1_cond_ln1_b", "L1_cond_wq", "L1_cond_wk", "L1_cond_wv", "L1_cond_wo",
        "L1_cond_wo_b", "L1_cond_ln2_w", "L1_cond_ln2_b", "L1_cond_fc1_w", "L1_cond_fc1_b",
        "L1_cond_fc2_w", "L1_cond_fc2_b", "L1_cond_ada_w", "L1_cond_ada_b"]


def kernel(**inputs):
    import numpy as np
    import concourse.bacc as bacc
    from concourse.bass_utils import run_bass_kernel_spmd

    nc = bacc.Bacc("TRN2", target_bir_lowering=False, num_devices=1)
    arrays, args = {}, []
    for name in _INS:
        a = np.ascontiguousarray(inputs[name])
        arrays[f"in_{name}"] = a
        args.append(nc.dram_tensor(f"in_{name}", a.shape, mybir.dt.from_np(a.dtype),
                                   kind="ExternalInput").ap())
    out = nc.dram_tensor("out", (BATCH, SEQ, C), F32, kind="ExternalOutput").ap()
    build(nc, *args, out)
    return run_bass_kernel_spmd(nc, [arrays], core_ids=[0]).results[0]["out"]
```
